# Optimizing a Trainium2 kernel written in Bass

```python
import numpy as np
import jax
import jax.numpy as jnp

def _softmax(x, axis=-1):
    return jax.nn.softmax(x, axis=axis)

def _gelu(x):
    return jax.nn.gelu(x, approximate=True)

def _silu(x):
    return jax.nn.silu(x)

def _sigmoid(x):
    return jax.nn.sigmoid(x)

def _layernorm(x, axis=-1, eps=1e-05):
    m = jnp.mean(x, axis=axis, keepdims=True)
    v = jnp.var(x, axis=axis, keepdims=True)
    return (x - m) / jnp.sqrt(v + eps)

def _scatter_add(tgt, idx, src, axis=0):
    return tgt.at[idx].add(src)

def _segment_sum(src, seg, n):
    return jax.ops.segment_sum(src, seg, n)
kernel_name = 'mk_seq_preln_d1_jaxref_r8_512240'

def setup_inputs(seed: int=0):
    np.random.seed(seed)
    _w = jnp.asarray

    def _L0_attn_setup():
        import math
        import jax, jax.numpy as jnp
        import numpy as np
        D_MODEL = 256
        NUM_HEADS = 16
        key = jax.random.key(seed)
        k1, k2, k3, k4, k5 = jax.random.split(key, 5)
        s = 1.0 / math.sqrt(D_MODEL)
        return {'in_features': jax.random.normal(k1, (2, 256, D_MODEL), dtype=jnp.float32), 'q_proj': jax.random.normal(k2, (D_MODEL, D_MODEL), dtype=jnp.float32) * s, 'k_proj': jax.random.normal(k3, (D_MODEL, D_MODEL), dtype=jnp.float32) * s, 'v_proj': jax.random.normal(k4, (D_MODEL, D_MODEL), dtype=jnp.float32) * s, 'o_proj': jax.random.normal(k5, (D_MODEL, D_MODEL), dtype=jnp.float32) * s}
    _L0_attn_in = _L0_attn_setup()

    def _L0_ffn_setup():
        import jax, jax.numpy as jnp
        import numpy as np
        K = 2
        SCALING = 16.0 / 16.0
        key = jax.random.key(seed)
        ks = jax.random.split(key, 7)
        B, T, D, O, E, R = (2, 512, 256, 256, 8, 16)
        return {'x': jax.random.normal(ks[0], (B, T, D), dtype=jnp.float32), 'W': jax.random.normal(ks[1], (O, D), dtype=jnp.float32) * (1.0 / np.sqrt(D)), 'b': jax.random.normal(ks[2], (O,), dtype=jnp.float32) * 0.02, 'lora_A': jax.random.normal(ks[3], (E, R, D), dtype=jnp.float32) * (1.0 / np.sqrt(D)), 'lora_B': jax.random.normal(ks[4], (E, O, R), dtype=jnp.float32) * 0.02, 'gate_w': jax.random.normal(ks[5], (E, D), dtype=jnp.float32) * 0.02, 'gate_b': jax.random.normal(ks[6], (E,), dtype=jnp.float32) * 0.02}
    _L0_ffn_in = _L0_ffn_setup()
    _d = {'L0_attn_in_features': _L0_attn_in['in_features'], 'L0_attn_q_proj': _L0_attn_in['q_proj'], 'L0_attn_k_proj': _L0_attn_in['k_proj'], 'L0_attn_v_proj': _L0_attn_in['v_proj'], 'L0_attn_o_proj': _L0_attn_in['o_proj'], 'L0_ffn_W': _L0_ffn_in['W'], 'L0_ffn_b': _L0_ffn_in['b'], 'L0_ffn_lora_A': _L0_ffn_in['lora_A'], 'L0_ffn_lora_B': _L0_ffn_in['lora_B'], 'L0_ffn_gate_w': _L0_ffn_in['gate_w'], 'L0_ffn_gate_b': _L0_ffn_in['gate_b']}
    _x0 = _d['L0_attn_in_features']
    _d['L0_attn_in_features'] = jax.random.normal(jax.random.fold_in(jax.random.key(seed), 1), (1, 2048, 256), dtype=_x0.dtype)
    del _x0
    return _d

def reference(L0_attn_in_features, L0_attn_q_proj, L0_attn_k_proj, L0_attn_v_proj, L0_attn_o_proj, L0_ffn_W, L0_ffn_b, L0_ffn_lora_A, L0_ffn_lora_B, L0_ffn_gate_w, L0_ffn_gate_b):

    def _L0_attn_ref(in_features, q_proj, k_proj, v_proj, o_proj):
        import math
        import jax, jax.numpy as jnp
        import numpy as np
        D_MODEL = 256
        NUM_HEADS = 16
        B, S, D = in_features.shape
        H = NUM_HEADS
        d_k = D // H

        def proj(W):
            return (in_features @ W.T).reshape(B, S, H, d_k).transpose(0, 2, 1, 3)
        Q, K, V = (proj(q_proj), proj(k_proj), proj(v_proj))
        scores = jnp.einsum('bhqd,bhkd->bhqk', Q, K) / math.sqrt(d_k)
        causal = jnp.triu(jnp.ones((S, S), dtype=bool), k=1)
        scores = jnp.where(causal, -jnp.inf, scores)
        attn = jax.nn.softmax(scores, axis=-1)
        out = jnp.einsum('bhqk,bhkd->bhqd', attn, V)
        out = out.transpose(0, 2, 1, 3).reshape(B, S, D)
        return out @ o_proj.T

    def _L0_ffn_ref(x, W, b, lora_A, lora_B, gate_w, gate_b):
        import jax, jax.numpy as jnp
        import numpy as np
        K = 2
        SCALING = 16.0 / 16.0
        orig_shape = x.shape
        D = orig_shape[-1]
        O = W.shape[0]
        x_flat = x.reshape(-1, D)
        base = x_flat @ W.T + b
        logits = x_flat @ gate_w.T + gate_b
        topk_logits, topk_idx = jax.lax.top_k(logits, K)
        gates = jax.nn.softmax(topk_logits, axis=-1)
        xA = jnp.einsum('nd,erd->ner', x_flat, lora_A)
        delta_all = jnp.einsum('ner,eor->neo', xA, lora_B)
        delta_topk = jnp.take_along_axis(delta_all, topk_idx[:, :, None], axis=1)
        lora_update = jnp.sum(delta_topk * gates[:, :, None], axis=1)
        out = base + SCALING * lora_update
        return out.reshape(*orig_shape[:-1], O)
    x = L0_attn_in_features
    x = x + _L0_attn_ref(_layernorm(x, axis=-1), L0_attn_q_proj, L0_attn_k_proj, L0_attn_v_proj, L0_attn_o_proj)
    x = x + _L0_ffn_ref(_layernorm(x, axis=-1), L0_ffn_W, L0_ffn_b, L0_ffn_lora_A, L0_ffn_lora_B, L0_ffn_gate_w, L0_ffn_gate_b)
    return x

_drawn_inputs = setup_inputs


def setup_inputs(seed=0):
    import zlib

    import numpy as np

    out = dict(_drawn_inputs(seed))
    spreads = {}
    factors = {'L0_ffn_b': 4.061, 'L0_ffn_gate_b': 6.441}
    for name, (base, spread) in spreads.items():
        noise = np.random.default_rng([zlib.crc32(name.encode()), seed]).standard_normal(out[name].shape)
        drawn = base * np.exp(spread * noise) if base else spread * noise
        out[name] = jnp.asarray(drawn.astype(out[name].dtype))
    for name, factor in factors.items():
        out[name] = (out[name] * factor).astype(out[name].dtype)
    return out
```

```python
from contextlib import ExitStack

import numpy as np

import concourse.bass as bass
from concourse import mybir

F32 = mybir.dt.float32
BF16 = mybir.dt.bfloat16
I32 = mybir.dt.int32
U32 = mybir.dt.uint32
ALU = mybir.AluOpType
ACT = mybir.ActivationFunctionType
AX_X = mybir.AxisListType.X

P = 128
S, D = 2048, 256
H, DK = 16, 16
E, R = 8, 16
EPS = 1e-5
TILES = S // P
CHUNK = 512
NCHUNK = S // CHUNK
TPC = CHUNK // P
QUAD = 4
NQUAD = H // QUAD
KH = D // P
FFN = D + E * R + E

Q_SLOTS = (0, 0, 0, 1, 1, 1, 2)
K_SLOTS = (0, 1, 2, 0, 1, 2, 0)
K_RUNS = ((0, 3), (3, 3), (6, 1))
STACK = DK * len(Q_SLOTS)
SHIFT_ROWS = 3
TAIL = P - STACK

BOUND, SHIFT = 40.0, 20.0
ROUNDING = 0.97
BIG = 3.0e38


def vary_lanes(n=32):
    return [(lane + n // 2) % n for lane in range(n)]


def transformer_block(nc, x, wqkv, wo, wffn, lora_b, biases, ident, ident_bf, masks, lane_scales, head_sum,
                      expert_ids, k_tail, q_tail, out):
    ctx = ExitStack()
    with ctx:
        def sb(name, shape, dt=F32):
            return ctx.enter_context(nc.sbuf_tensor(name, shape, dt))

        def bank(name, shape, dt=F32):
            return ctx.enter_context(nc.psum_tensor(name, shape, dt))

        def sem(name):
            return ctx.enter_context(nc.semaphore(name))

        parts_dram = nc.dram_tensor("parts_dram", (NCHUNK, 2, 3, KH, P, CHUNK), BF16, kind="Internal").ap()
        shift_dram = nc.dram_tensor("shift_dram", (NCHUNK, H, SHIFT_ROWS * TPC, P), BF16, kind="Internal").ap()

        x_sb = sb("x_sb", [P, TILES, D])
        wqkv_sb = sb("wqkv_sb", [P, KH, 3 * D])
        wo_sb = sb("wo_sb", [P, KH, D])
        wffn_sb = sb("wffn_sb", [P, KH, FFN])
        lora_b_sb = sb("lora_b_sb", [P, D])
        biases_sb = sb("biases_sb", [P, D + E])
        ident_sb = sb("ident_sb", [P, P])
        ident_bf_sb = sb("ident_bf_sb", [P, P], BF16)
        masks_sb = sb("masks_sb", [P, 2, P])
        lane_scales_sb = sb("lane_scales_sb", [P, 3, NQUAD])
        head_sum_sb = sb("head_sum_sb", [P, H], BF16)
        expert_ids_sb = sb("expert_ids_sb", [P, E])
        hold_cell = sb("hold_cell", [1, 1])
        minus_half = sb("minus_half", [P, 1])
        k_stack = sb("k_stack", [P, H, S], BF16)
        q_stack = sb("q_stack", [P, 2, H, CHUNK], BF16)
        v_all = sb("v_all", [P, TILES, H, 32])
        attn = sb("attn", [P, 2, KH, CHUNK])

        v_ring = sb("v_ring", [P, 4, QUAD, 32])
        probs = sb("probs", [P, 2, QUAD, CHUNK])
        acc_sb = sb("acc_sb", [P, CHUNK])
        sums = sb("sums", [P, CHUNK])
        bn1 = sb("bn1", [P, 6])
        mv1 = sb("mv1", [P, 2])
        ve1 = sb("ve1", [P, 1])
        rstd1 = sb("rstd1", [P, 1])
        xln = sb("xln", [P, D])
        xT = sb("xT", [P, KH, P])
        parts = sb("parts", [P, 2, 3, KH, P], BF16)
        rest1 = sb("rest1", [P, 2, KH, P])
        clamped = sb("clamped", [P, 2, KH, P], BF16)
        norms = sb("norms", [H, 2, TILES])
        norm_max = sb("norm_max", [H, 2])
        bound_sq = sb("bound_sq", [32, 32])
        bound_row = sb("bound_row", [32, 32])
        bound_max = sb("bound_max", [1, 1])
        is_bounded = sb("is_bounded", [1, NCHUNK], I32)
        row_max = sb("row_max", [P, 8])
        masked = sb("masked", [P, P])
        shift = sb("shift", [P, TPC])
        shift_rest = sb("shift_rest", [P, TPC])
        shift_parts = sb("shift_parts", [P, SHIFT_ROWS, TPC], BF16)
        shift_rows = sb("shift_rows", [SHIFT_ROWS * TPC, P], BF16)
        attn_t = sb("attn_t", [P, KH, P])
        y = sb("y", [P, D])
        yb = sb("yb", [P, D])
        bn2 = sb("bn2", [P, 6])
        mv2 = sb("mv2", [P, 2])
        ve2 = sb("ve2", [P, 1])
        rstd2 = sb("rstd2", [P, 1])
        yln = sb("yln", [P, D])
        yT = sb("yT", [P, KH, P])
        logits = sb("logits", [P, E])
        top = sb("top", [P, 8])
        top_at = sb("top_at", [P, 8], U32)
        top_id = sb("top_id", [P, 2])
        top_gap = sb("top_gap", [P, 1])
        exp_gap = sb("exp_gap", [P, 1])
        gate_den = sb("gate_den", [P, 1])
        gate_of = sb("gate_of", [P, 2])
        gates2 = sb("gates2", [P, 2, E])
        gates = sb("gates", [P, E])
        gated = sb("gated", [P, E, R])
        gatedT = sb("gatedT", [P, P])
        result = sb("result", [P, D])

        scores = [bank(f"scores{a}", [P, 2, CHUNK]) for a in range(2)]
        acc = bank("acc", [P, CHUNK])
        pre_a = bank("pre_a", [P, 2, D])
        pre_b = bank("pre_b", [P, 2, KH, P])
        post = bank("post", [P, CHUNK])

        weights_in = sem("weights_in")
        x_in = [sem(f"x_in{c}") for c in range(NCHUNK)]
        consts_in = sem("consts_in")
        post_weights_in = sem("post_weights_in")
        tails_in = sem("tails_in")
        const_set = sem("const_set")
        stats1 = sem("stats1")
        rstd1_ready = sem("rstd1_ready")
        xln_ready = sem("xln_ready")
        xT_psum = sem("xT_psum")
        xT_ready = sem("xT_ready")
        qk_psum = sem("qk_psum")
        v_psum = sem("v_psum")
        v_stored = sem("v_stored")
        split = sem("split")
        low_ready = sem("low_ready")
        norm_psum = sem("norm_psum")
        norm_read = sem("norm_read")
        parts_out = sem("parts_out")
        stacks_in = sem("stacks_in")
        bound_step = sem("bound_step")
        gen_scores = [sem(f"gen_scores{c}") for c in range(NCHUNK)]
        gen_max = [sem(f"gen_max{c}") for c in range(NCHUNK)]
        gen_read = [sem(f"gen_read{c}") for c in range(NCHUNK)]
        gen_turned = [sem(f"gen_turned{c}") for c in range(NCHUNK)]
        gen_rows = [sem(f"gen_rows{c}") for c in range(NCHUNK)]
        gen_out = [sem(f"gen_out{c}") for c in range(NCHUNK)]
        gen_in = [sem(f"gen_in{c}") for c in range(NCHUNK)]
        scores_ready = sem("scores_ready")
        exp_done = sem("exp_done")
        causal_done = sem("causal_done")
        v_ready = sem("v_ready")
        pv_done = sem("pv_done")
        acc_read = sem("acc_read")
        norm_step = sem("norm_step")
        attn_t_ready = sem("attn_t_ready")
        o_psum = sem("o_psum")
        stats2 = sem("stats2")
        rstd2_ready = sem("rstd2_ready")
        yb_ready = sem("yb_ready")
        yln_ready = sem("yln_ready")
        yT_psum = sem("yT_psum")
        yT_ready = sem("yT_ready")
        ffn_psum = sem("ffn_psum")
        route = sem("route")
        gap_exp = sem("gap_exp")
        gatedT_psum = sem("gatedT_psum")
        gatedT_ready = sem("gatedT_ready")
        out_psum = sem("out_psum")
        result_ready = sem("result_ready")
        result_out = sem("result_out")

        STATS1, SPLIT, BOUND_STEPS, NORM, STATS2, ROUTE = 3, 5, 5, 5, 4, 12
        STACK_DMAS = len(Q_SLOTS) + len(K_RUNS)

        periods = [TPC * (c + 1) for c in range(NCHUNK)]
        first_period = [NQUAD * sum(periods[:c]) for c in range(NCHUNK)]

        def span(c, kb):
            return max(0, kb - TPC * c) * P

        def pre_slots(c):
            return {} if c == NCHUNK - 1 else ({2: "turn", 3: "project", 4: "norm"} if c == 0
                                               else {2: "turn", 3: "project", 5: "norm"})

        def post_slots(c):
            return {} if c == 0 else {1: "o", 3: "turn", 4: "ffn", 6: "turn_gated", 7: "lora"}

        block = ctx.enter_context(nc.Block())

        @block.sync
        def _(sp):
            sp.dma_start(x_sb[:, 0:TPC, :], x[:, 0:TPC, :]).then_inc(x_in[0], 16)
            sp.dma_start(ident_sb[:], ident).then_inc(consts_in, 16)
            sp.dma_start(wqkv_sb[:], wqkv).then_inc(weights_in, 16)
            sp.dma_start(head_sum_sb[:], head_sum).then_inc(consts_in, 16)
            sp.dma_start(masks_sb[:], masks).then_inc(consts_in, 16)
            sp.dma_start(lane_scales_sb[:], lane_scales).then_inc(consts_in, 16)
            sp.dma_start(ident_bf_sb[:], ident_bf).then_inc(consts_in, 16)
            for par in range(2):
                sp.dma_start(q_stack[STACK:P, par], q_tail).then_inc(tails_in, 16)
            for c in range(NCHUNK):
                sp.dma_start(k_stack[STACK:P, :, c * CHUNK:(c + 1) * CHUNK], k_tail).then_inc(tails_in, 16)
            for c in range(1, NCHUNK):
                sp.dma_start(x_sb[:, c * TPC:(c + 1) * TPC, :], x[:, c * TPC:(c + 1) * TPC, :]).then_inc(x_in[c], 16)
            sp.dma_start(wo_sb[:], wo).then_inc(post_weights_in, 16)
            sp.dma_start(wffn_sb[:], wffn).then_inc(post_weights_in, 16)
            sp.dma_start(lora_b_sb[:], lora_b).then_inc(post_weights_in, 16)
            sp.dma_start(biases_sb[:], biases).then_inc(result_out, 16)
            sp.dma_start(expert_ids_sb[:], expert_ids).then_inc(post_weights_in, 16)

            def store_parts(c, i):
                g = c * TPC + i
                sp.wait_ge(low_ready, g + 1)
                sp.wait_ge(split, SPLIT * g + 4)
                sp.dma_start(parts_dram[c, :, :, :, :, bass.ds(i * P, P)].rearrange("k s m p t -> p (k s m) t"),
                             parts[:].rearrange("p k s m t -> p (k s m) t")).then_inc(parts_out, 16)

            def load_stacks(c, quad):
                rows = parts_dram[c].rearrange("k s m (d h) t -> k (s m d) h t", h=H)
                heads = bass.ds(quad * QUAD if isinstance(quad, int) else sp.snap(quad * QUAD), QUAD)
                if c > 0 or not isinstance(quad, int):
                    sp.wait_ge(stacks_in, 16 * STACK_DMAS * (NQUAD * c + quad))
                for n, part in enumerate(Q_SLOTS):
                    sp.dma_start(q_stack[n * DK:(n + 1) * DK, c % 2, heads, :],
                                 rows[0, part * DK:(part + 1) * DK, heads, :]).then_inc(stacks_in, 16)
                for n, k in K_RUNS:
                    sp.dma_start(k_stack[n * DK:(n + k) * DK, heads, c * CHUNK:(c + 1) * CHUNK],
                                 rows[1, 0:k * DK, heads, :]).then_inc(stacks_in, 16)

            def store_shifts(c):
                sp.wait_ge(stacks_in, 16 * STACK_DMAS * NQUAD * (c + 1))
                sp.wait_ge(tails_in, 16 * (2 + NCHUNK))
                with sp.Fori(0, H) as h:
                    sp.wait_ge(gen_rows[c], h + 1)
                    sp.dma_start(shift_dram[c, h], shift_rows[:]).then_inc(gen_out[c], 16)
                    sp.wait_ge(gen_out[c], 16 * (h + 1))
                    sp.dma_start(q_stack[STACK:STACK + SHIFT_ROWS, c % 2, h, :],
                                 shift_dram[c, h].rearrange("(s i) t -> s (i t)", s=SHIFT_ROWS)
                                 ).then_inc(gen_in[c], 16)

            with sp.Fori(0, TPC) as i:
                store_parts(0, i)
            for c in range(NCHUNK):
                sp.wait_ge(parts_out, 16 * TPC * (c + 1))
                load_stacks(c, 0)
                sp.wait_ge(bound_step, BOUND_STEPS * (c + 1))
                bounded = sp.value_load(is_bounded[0:1, c:c + 1], min_val=0, max_val=1)
                with sp.If(bounded == 0):
                    with sp.Fori(1, NQUAD) as quad:
                        load_stacks(c, quad)
                    store_shifts(c)
                    if c + 1 < NCHUNK:
                        with sp.Fori(0, TPC) as i:
                            store_parts(c + 1, i)
                with sp.If(bounded == 1):
                    with sp.Fori(1, NQUAD) as quad:
                        load_stacks(c, quad)
                        if c + 1 < NCHUNK:
                            store_parts(c + 1, quad - 1)
                    if c + 1 < NCHUNK:
                        store_parts(c + 1, TPC - 1)
            sp.wait_ge(parts_out, 16 * TILES)
            sp.wait_ge(result_out, 16 * (TILES + 1))

        @block.tensor
        def _(pe):
            def turn_x(g):
                pe.wait_ge(xln_ready, g + 1)
                for k in range(KH):
                    t = pe.transpose(pre_a[:, 0, k * P:(k + 1) * P], xln[:, k * P:(k + 1) * P], ident_sb[:])
                t.then_inc(xT_psum, 1)

            def project(g):
                pe.wait_ge(xT_ready, g + 1)
                for n in range(2 * KH):
                    for k in range(KH):
                        m = pe.matmul(pre_b[:, n // KH, n % KH, :], wqkv_sb[:, k, n * P:(n + 1) * P], xT[:, k, :],
                                      start=(k == 0), stop=(k == KH - 1))
                m.then_inc(qk_psum, 1)
                for k in range(KH):
                    m = pe.matmul(pre_a[:, 1, :], xT[:, k, :], wqkv_sb[:, k, 2 * D:3 * D],
                                  start=(k == 0), stop=(k == KH - 1))
                m.then_inc(v_psum, 1)

            def sum_squares(g):
                pe.wait_ge(split, SPLIT * (g + 1))
                for k in range(KH):
                    m = pe.matmul(pre_b[0:H, :, 0, :], head_sum_sb[:], clamped[:, :, k, :],
                                  start=(k == 0), stop=(k == KH - 1))
                m.then_inc(norm_psum, 1)

            PRE = {"turn": turn_x, "project": project, "norm": sum_squares}

            def o_proj(g, in_quads):
                pe.wait_ge(attn_t_ready, g + 1)
                if not in_quads:
                    pe.wait_ge(result_ready, g)
                for k in range(KH):
                    m = pe.matmul(post[:, 0:D], attn_t[:, k, :], wo_sb[:, k, :], start=(k == 0), stop=(k == KH - 1))
                m.then_inc(o_psum, 1)

            def turn_y(g):
                pe.wait_ge(yln_ready, g + 1)
                for k in range(KH):
                    t = pe.transpose(post[:, D + k * P:D + (k + 1) * P], yln[:, k * P:(k + 1) * P], ident_sb[:])
                t.then_inc(yT_psum, 1)

            def ffn(g):
                pe.wait_ge(yT_ready, g + 1)
                for k in range(KH):
                    m = pe.matmul(post[:, 0:FFN], yT[:, k, :], wffn_sb[:, k, :], start=(k == 0), stop=(k == KH - 1),
                                  skip_group_check=True)
                m.then_inc(ffn_psum, 1)

            def turn_gated(g, v_tiles):
                pe.wait_ge(route, ROUTE * (g + 1))
                pe.wait_ge(v_stored, v_tiles)
                pe.transpose(pre_a[:, 0, 0:P], gated[:].rearrange("p e r -> p (e r)"), ident_sb[:]
                             ).then_inc(gatedT_psum, 1)

            def lora(g):
                pe.wait_ge(gatedT_ready, g + 1)
                pe.matmul(post[:, 0:D], gatedT[:], lora_b_sb[:], start=False, stop=True,
                          skip_group_check=True).then_inc(out_psum, 1)

            def post_stage(name, g, v_tiles, in_quads=True):
                if name == "o":
                    o_proj(g, in_quads)
                elif name == "turn":
                    turn_y(g)
                elif name == "ffn":
                    ffn(g)
                elif name == "turn_gated":
                    turn_gated(g, v_tiles)
                else:
                    lora(g)

            def row_maxima(c):
                with pe.Fori(0, H) as h:
                    for i in range(TPC):
                        if i > 0:
                            pe.wait_ge(gen_read[c], TPC * h + i)
                        lhs = q_stack[0:STACK, c % 2, h, i * P:(i + 1) * P]
                        for kc in range(c + 1):
                            n = CHUNK if kc < c else (i + 1) * P
                            m = pe.matmul(scores[kc // 2][:, kc % 2, 0:n], lhs,
                                          k_stack[0:STACK, h, kc * CHUNK:kc * CHUNK + n], start=True, stop=True)
                        m.then_inc(gen_scores[c], 1)
                    pe.wait_ge(gen_max[c], h + 1)
                    pe.transpose(post[0:SHIFT_ROWS * TPC, 0:P // 2].bitcast(BF16),
                                 shift_parts[:].rearrange("p s i -> p (s i)"), ident_bf_sb[:]
                                 ).then_inc(gen_turned[c], 1)
                pe.wait_ge(gen_in[c], 16 * H)

            def attend(c, i):
                last = periods[c] - 1
                base = first_period[c] + i * periods[c]
                quad_no = NQUAD * c + i

                def qk(kb):
                    n, lo = base + kb, span(c, kb)
                    for a in range(2):
                        if kb > 0:
                            pe.wait_ge(exp_done, 2 * n + a - 1)
                        for j in range(2):
                            head = i * QUAD + 2 * a + j
                            m = pe.matmul(scores[a][:, j, lo:CHUNK], k_stack[:, head, kb * P:(kb + 1) * P],
                                          q_stack[:, c % 2, head, lo:CHUNK], start=True, stop=True)
                        m.then_inc(scores_ready, 1)

                def pv(kb):
                    n, lo = base + kb, span(c, kb)
                    pe.wait_ge(exp_done, 2 * n + 2)
                    pe.wait_ge(v_ready, n + 1)
                    if kb >= TPC * c:
                        pe.wait_ge(causal_done, TPC * quad_no + kb - TPC * c + 1)
                    if kb == 0:
                        pe.wait_ge(acc_read, quad_no + 1)
                    for j in range(QUAD):
                        m = pe.matmul(acc[32 * j:32 * j + 32, lo:CHUNK], v_ring[:, kb % 4, j, :],
                                      probs[:, kb % 2, j, lo:CHUNK], start=(kb == 0), stop=(kb == last),
                                      tile_position=(0, 32 * j))
                    m.then_inc(pv_done, 1)

                pre, post_ = pre_slots(c), post_slots(c)

                def slot(k):
                    g_pre, g_post = TPC * (c + 1) + i, TPC * (c - 1) + i
                    if k in pre:
                        PRE[pre[k]](g_pre)
                    if k in post_:
                        done = g_pre + 1 if c < NCHUNK - 1 else TILES
                        post_stage(post_[k], g_post, done)

                for kb in range(last + 1):
                    qk(kb)
                    if kb > 0:
                        pv(kb - 1)
                    slot(kb)
                slot(last + 1)
                pv(last)

            pe.wait_ge(weights_in, 16)
            pe.wait_ge(const_set, 1)
            pe.wait_ge(consts_in, 16 * 5)
            with pe.Fori(0, TPC) as i:
                turn_x(i)
                project(i)
                sum_squares(i)
            pe.wait_ge(tails_in, 16 * (2 + NCHUNK))
            for c in range(NCHUNK):
                pe.wait_ge(bound_step, BOUND_STEPS * (c + 1))
                bounded = pe.value_load(is_bounded[0:1, c:c + 1], min_val=0, max_val=1)
                with pe.If(bounded == 0):
                    pe.wait_ge(stacks_in, 16 * STACK_DMAS * NQUAD * (c + 1))
                    if c > 0:
                        pe.wait_ge(exp_done, 2 * first_period[c])
                    row_maxima(c)
                if c == 1:
                    pe.wait_ge(post_weights_in, 16 * 4)
                with pe.Fori(0, NQUAD) as i:
                    pe.wait_ge(stacks_in, 16 * STACK_DMAS * (NQUAD * c + i + 1))
                    attend(c, i)
            with pe.Fori(0, TPC) as i:
                g = TILES - TPC + i
                for name in ("o", "turn", "ffn", "turn_gated", "lora"):
                    post_stage(name, g, TILES, in_quads=False)

        @block.scalar
        def _(act):
            def exp_gap_of(g):
                act.wait_ge(route, ROUTE * g + 4)
                act.activation(exp_gap[:], top_gap[:], ACT.Exp).then_inc(gap_exp, 1)

            def store(g):
                act.wait_ge(result_ready, g + 1)
                act.dma_start(out[g], result[:]).then_inc(result_out, 16)

            for c in range(NCHUNK):
                with act.Fori(0, NQUAD) as i:
                    base = first_period[c] + i * periods[c]
                    for kb in range(periods[c]):
                        n, lo = base + kb, span(c, kb)
                        for a in range(2):
                            act.wait_ge(scores_ready, 2 * n + a + 1)
                            act.activation(probs[:, kb % 2, 2 * a:2 * a + 2, lo:CHUNK], scores[a][:, :, lo:CHUNK],
                                           ACT.Exp).then_inc(exp_done, 1)
                        if post_slots(c).get(kb - 1) == "ffn":
                            exp_gap_of(TPC * (c - 1) + i)
                    if c > 0:
                        store(TPC * (c - 1) + i)
            with act.Fori(0, TPC) as i:
                exp_gap_of(TILES - TPC + i)
                store(TILES - TPC + i)

        @block.vector
        def _(dve):
            dve.memset(minus_half[:], -0.5)
            dve.memset(bound_sq[:], 0.0)
            dve.memset(attn[:].rearrange("p c a t -> p (c a t)"), 0.0).then_inc(acc_read, 1)
            dve.memset(v_all[:].rearrange("p t h d -> p (t h d)"), 1.0)
            dve.wait_ge(weights_in, 16)
            dve.tensor_scalar(wqkv_sb[:, :, 0:D], wqkv_sb[:, :, 0:D], float(DK) ** -0.5, None,
                              ALU.mult).then_inc(const_set, 1)
            dve.wait_ge(const_set, 1)
            dve.wait_ge(consts_in, 16 * 5)

            def hold_here():
                dve.memset(hold_cell[:], 0.0)

            def normalise_x(g):
                dve.bn_stats(bn1[:], x_sb[:, g, :]).then_inc(stats1, 1)
                dve.wait_ge(stats1, STATS1 * g + 1)
                hold_here()
                dve.bn_aggr(mv1[:], bn1[:]).then_inc(stats1, 1)
                dve.wait_ge(stats1, STATS1 * g + 2)
                dve.tensor_scalar(ve1[:], mv1[:, 1:2], EPS, None, ALU.add).then_inc(stats1, 1)
                dve.wait_ge(rstd1_ready, g + 1)
                dve.tensor_scalar(xln[:], x_sb[:, g, :], mv1[:, 0:1], rstd1[:], ALU.subtract,
                                  ALU.mult).then_inc(xln_ready, 1)

            def store_xT(g):
                dve.wait_ge(xT_psum, g + 1)
                dve.tensor_copy(xT[:].rearrange("p k t -> p (k t)"), pre_a[:, 0, :]).then_inc(xT_ready, 1)

            def split_qk(g):
                base = SPLIT * g
                dve.wait_ge(qk_psum, g + 1)
                if not (isinstance(g, int) and g == 0):
                    dve.wait_ge(low_ready, g)
                    dve.wait_ge(parts_out, 16 * g)
                high, middle = parts[:, :, 0], parts[:, :, 1]
                dve.tensor_copy(high, pre_b[:]).then_inc(split, 1)
                dve.wait_ge(split, base + 1)
                dve.tensor_tensor(rest1[:], pre_b[:], high, ALU.subtract).then_inc(split, 1)
                dve.tensor_scalar(clamped[:], high, 1e15, -1e15, ALU.min, ALU.max).then_inc(split, 1)
                dve.wait_ge(split, base + 3)
                dve.tensor_copy(middle, rest1[:]).then_inc(split, 1)
                dve.tensor_tensor(clamped[:], clamped[:], clamped[:], ALU.mult).then_inc(split, 1)

            def store_v(g):
                dve.wait_ge(v_psum, g + 1)
                v_in = pre_a[:, 1, :].rearrange("p (a b h d) -> p a b h d", a=2, b=2, h=QUAD)
                v_out = v_all[:, g].rearrange("p (a b h) d -> p a b h d", a=2, b=2)
                dve.tensor_copy(v_out[:, :, 0, :, 0:DK], v_in[:, :, 0])
                dve.tensor_copy(v_out[:, :, 1, :, DK:2 * DK], v_in[:, :, 1]).then_inc(v_stored, 1)

            def read_norms(g):
                dve.wait_ge(norm_psum, g + 1)
                dve.tensor_reduce(norms[:, :, bass.ds(g, 1)], pre_b[0:H, :, 0, :], AX_X, ALU.max).then_inc(norm_read, 1)

            def decide_bound(c):
                base = BOUND_STEPS * c
                dve.wait_ge(norm_read, TPC * (c + 1))
                dve.tensor_reduce(norm_max[:], norms[:, :, 0:TPC * (c + 1)], AX_X, ALU.max).then_inc(bound_step, 1)
                dve.wait_ge(bound_step, base + 1)
                dve.tensor_scalar(bound_sq[0:H, 0:1], norm_max[:, 0:1], norm_max[:, 1:2], None,
                                  ALU.mult).then_inc(bound_step, 1)
                dve.wait_ge(bound_step, base + 2)
                dve.transpose(bound_row[:], bound_sq[:]).then_inc(bound_step, 1)
                dve.wait_ge(bound_step, base + 3)
                dve.tensor_reduce(bound_max[:], bound_row[0:1, 0:H], AX_X, ALU.max).then_inc(bound_step, 1)
                dve.wait_ge(bound_step, base + 4)
                dve.tensor_scalar(is_bounded[:, c:c + 1], bound_max[:], BOUND * BOUND * ROUNDING, None,
                                  ALU.is_le).then_inc(bound_step, 1)
                dve.wait_ge(bound_step, base + 5)

            def shifts(c):
                step = 0
                with dve.Fori(0, H) as h:
                    for i in range(TPC):
                        done = h * (TPC * GEN_STEPS + GEN_SPLIT) + i * GEN_STEPS
                        step = gen_step[c]
                        dve.memset(row_max[:], -BIG).then_inc(step, 1)
                        dve.wait_ge(gen_scores[c], TPC * h + i + 1)
                        dve.wait_ge(step, done + 1)
                        dve.tensor_tensor(masked[:], scores[c // 2][:, c % 2, i * P:(i + 1) * P], masks_sb[:, 1, :],
                                          ALU.min).then_inc(step, 1)
                        for kc in range(c):
                            dve.tensor_reduce(row_max[:, kc:kc + 1], scores[kc // 2][:, kc % 2, :], AX_X, ALU.max)
                        if i > 0:
                            dve.tensor_reduce(row_max[:, 4:5], scores[c // 2][:, c % 2, 0:i * P], AX_X, ALU.max)
                        dve.wait_ge(step, done + 2)
                        dve.tensor_reduce(row_max[:, 5:6], masked[:], AX_X, ALU.max).then_inc(gen_read[c], 1)
                        dve.wait_ge(gen_read[c], TPC * h + i + 1)
                        dve.tensor_reduce(masked[:, 0:1], row_max[:], AX_X, ALU.max).then_inc(step, 1)
                        dve.wait_ge(step, done + 3)
                        dve.tensor_scalar(shift[:, i:i + 1], masked[:, 0:1], -1.0, None, ALU.mult).then_inc(step, 1)
                    done = h * (TPC * GEN_STEPS + GEN_SPLIT) + TPC * GEN_STEPS
                    dve.wait_ge(step, done)
                    dve.tensor_copy(shift_parts[:, 0], shift[:]).then_inc(step, 1)
                    dve.wait_ge(step, done + 1)
                    dve.tensor_tensor(shift_rest[:], shift[:], shift_parts[:, 0], ALU.subtract).then_inc(step, 1)
                    dve.wait_ge(step, done + 2)
                    dve.tensor_copy(shift_parts[:, 1], shift_rest[:]).then_inc(step, 1)
                    dve.wait_ge(step, done + 3)
                    dve.tensor_tensor(shift_parts[:, 2], shift_rest[:], shift_parts[:, 1],
                                      ALU.subtract).then_inc(gen_max[c], 1)
                    dve.wait_ge(gen_turned[c], h + 1)
                    dve.tensor_copy(shift_rows[:], post[0:SHIFT_ROWS * TPC, 0:P // 2].bitcast(BF16)
                                    ).then_inc(gen_rows[c], 1)
                    dve.wait_ge(gen_out[c], 16 * (h + 1))

            def clear_later_keys(c, quad_no, n, j, slot):
                dve.wait_ge(exp_done, 2 * n + 2)
                tile = probs[:, slot, :, j * P:(j + 1) * P]
                mask = masks_sb[:, 0:1, :].to_broadcast([P, QUAD, P])
                dve.tensor_tensor(tile, tile, mask, ALU.min).then_inc(causal_done, 1)

            def divide(c, i):
                quad_no = NQUAD * c + i
                base = NORM * quad_no
                dve.wait_ge(pv_done, first_period[c] + (i + 1) * periods[c])
                dve.tensor_copy(acc_sb[:], acc[:]).then_inc(acc_read, 1)
                dve.wait_ge(acc_read, quad_no + 2)
                hold_here()
                dve.stream_shuffle(sums[:], acc_sb[:], vary_lanes()).then_inc(norm_step, 1)
                dve.wait_ge(norm_step, base + 1)
                v_lane, other, second = (lane_scales_sb[:, n, bass.ds(i, 1)] for n in range(3))
                dve.tensor_scalar(sums[:], sums[:], v_lane, other, ALU.mult, ALU.add).then_inc(norm_step, 1)
                dve.wait_ge(norm_step, base + 2)
                dve.reciprocal(sums[:], sums[:]).then_inc(norm_step, 1)
                dve.wait_ge(norm_step, base + 3)
                dve.scalar_tensor_tensor(out=acc_sb[:], in0=acc_sb[:], scalar=v_lane, in1=sums[:],
                                         op0=ALU.mult, op1=ALU.mult).then_inc(norm_step, 1)
                dve.wait_ge(norm_step, base + 4)
                target = attn[:, c % 2, :, :].rearrange("p a t -> p (a t)")[:, bass.ds((i // 2) * CHUNK, CHUNK)]
                dve.scalar_tensor_tensor(out=target, in0=target, scalar=second, in1=acc_sb[:],
                                         op0=ALU.mult, op1=ALU.add).then_inc(norm_step, 1)

            def residual_and_stats(g):
                base = STATS2 * g
                dve.wait_ge(o_psum, g + 1)
                dve.tensor_tensor(y[:], post[:, 0:D], x_sb[:, g, :], ALU.add).then_inc(stats2, 1)
                dve.wait_ge(stats2, base + 1)
                dve.bn_stats(bn2[:], y[:]).then_inc(stats2, 1)
                dve.wait_ge(stats2, base + 2)
                hold_here()
                dve.bn_aggr(mv2[:], bn2[:]).then_inc(stats2, 1)
                dve.wait_ge(stats2, base + 3)
                dve.tensor_scalar(ve2[:], mv2[:, 1:2], EPS, None, ALU.add).then_inc(stats2, 1)
                dve.wait_ge(rstd2_ready, g + 1)
                dve.tensor_scalar(yln[:], y[:], mv2[:, 0:1], rstd2[:], ALU.subtract, ALU.mult).then_inc(yln_ready, 1)

            def store_yT(g):
                dve.wait_ge(yT_psum, g + 1)
                dve.tensor_copy(yT[:].rearrange("p k t -> p (k t)"), post[:, D:2 * D]).then_inc(yT_ready, 1)

            def route_tokens(g):
                base = ROUTE * g
                dve.wait_ge(result_out, 16)
                dve.wait_ge(ffn_psum, g + 1)
                dve.tensor_tensor(logits[:], post[:, D + E * R:FFN], biases_sb[:, D:D + E], ALU.add).then_inc(route, 1)
                dve.wait_ge(route, base + 1)
                hold_here()
                dve.max(top[:], logits[:]).then_inc(route, 1)
                dve.wait_ge(route, base + 2)
                hold_here()
                dve.max_index(top_at[:], top[:], logits[:]).then_inc(route, 1)
                dve.tensor_scalar(top_gap[:], top[:, 1:2], top[:, 0:1], None, ALU.subtract).then_inc(route, 1)
                dve.wait_ge(route, base + 3)
                dve.tensor_copy(top_id[:], top_at[:, 0:2]).then_inc(route, 1)
                dve.wait_ge(gap_exp, g + 1)
                dve.tensor_scalar(gate_den[:], exp_gap[:], 1.0, None, ALU.add).then_inc(route, 1)
                dve.wait_ge(route, base + 6)
                dve.reciprocal(gate_of[:, 0:1], gate_den[:]).then_inc(route, 1)
                dve.wait_ge(route, base + 7)
                dve.tensor_scalar(gate_of[:, 1:2], gate_of[:, 0:1], exp_gap[:], None, ALU.mult).then_inc(route, 1)
                dve.wait_ge(route, base + 8)
                for n in range(2):
                    dve.tensor_scalar(gates2[:, n, :], expert_ids_sb[:], top_id[:, n:n + 1], gate_of[:, n:n + 1],
                                      ALU.is_equal, ALU.mult).then_inc(route, 1)
                dve.wait_ge(route, base + 10)
                dve.tensor_tensor(gates[:], gates2[:, 0, :], gates2[:, 1, :], ALU.add).then_inc(route, 1)
                dve.wait_ge(route, base + 11)
                dve.tensor_tensor(gated[:], post[:, D:D + E * R].rearrange("p (e r) -> p e r", e=E),
                                  gates[:].unsqueeze(2).to_broadcast([P, E, R]), ALU.mult).then_inc(route, 1)

            def store_gatedT(g):
                dve.wait_ge(gatedT_psum, g + 1)
                dve.tensor_copy(gatedT[:], pre_a[:, 0, 0:P]).then_inc(gatedT_ready, 1)

            def finish(g):
                dve.wait_ge(out_psum, g + 1)
                dve.wait_ge(yb_ready, g + 1)
                dve.wait_ge(result_out, 16 * (g + 1))
                dve.tensor_tensor(result[:], post[:, 0:D], yb[:], ALU.add).then_inc(result_ready, 1)

            POST = {"o": residual_and_stats, "turn": store_yT, "ffn": route_tokens, "turn_gated": store_gatedT,
                    "lora": finish}

            GEN_STEPS, GEN_SPLIT = 4, 3
            gen_step = [sem(f"gen_step{c}") for c in range(NCHUNK)]

            dve.wait_ge(x_in[0], 16)
            def prepare(g):
                normalise_x(g)
                store_xT(g)
                split_qk(g)
                store_v(g)
                read_norms(g)

            prepare(0)
            with dve.Fori(1, TPC) as i:
                prepare(i)
            for c in range(NCHUNK):
                decide_bound(c)
                bounded = dve.value_load(is_bounded[0:1, c:c + 1], min_val=0, max_val=1)
                with dve.If(bounded == 0):
                    shifts(c)
                if c + 1 < NCHUNK:
                    dve.wait_ge(x_in[c + 1], 16)
                if c == 1:
                    dve.wait_ge(post_weights_in, 16 * 4)
                pre, post_ = pre_slots(c), post_slots(c)
                with dve.Fori(0, NQUAD) as i:
                    g_pre, g_post = TPC * (c + 1) + i, TPC * (c - 1) + i
                    if pre:
                        normalise_x(g_pre)
                    for k in range(periods[c] + 1):
                        if TPC * c <= k < periods[c]:
                            clear_later_keys(c, NQUAD * c + i, first_period[c] + i * periods[c] + k, k - TPC * c,
                                             k % 2)
                        if pre.get(k) == "turn":
                            store_xT(g_pre)
                        elif pre.get(k) == "project":
                            split_qk(g_pre)
                            store_v(g_pre)
                        elif pre.get(k) == "norm":
                            read_norms(g_pre)
                        if k in post_:
                            POST[post_[k]](g_post)
                    divide(c, i)
            with dve.Fori(0, TPC) as i:
                for name in ("o", "turn", "ffn", "turn_gated", "lora"):
                    POST[name](TILES - TPC + i)

        @block.gpsimd
        def _(pool):
            def rstd_x(g):
                pool.wait_ge(stats1, STATS1 * (g + 1))
                pool.tensor_tensor(rstd1[:], ve1[:], minus_half[:], ALU.pow).then_inc(rstd1_ready, 1)

            def low_parts(g):
                pool.wait_ge(split, SPLIT * g + 4)
                pool.tensor_tensor(parts[:, :, 2], rest1[:], parts[:, :, 1], ALU.subtract).then_inc(low_ready, 1)

            def gather_attention(g, c, i):
                pool.wait_ge(norm_step, NORM * NQUAD * (c + 1))
                pool.tensor_copy(attn_t[:], attn[:, c % 2, :, bass.ds(i * P, P)]).then_inc(attn_t_ready, 1)

            def rstd_y(g):
                pool.wait_ge(stats2, STATS2 * (g + 1))
                pool.tensor_tensor(rstd2[:], ve2[:], minus_half[:], ALU.pow).then_inc(rstd2_ready, 1)
                pool.tensor_tensor(yb[:], y[:], biases_sb[:, 0:D], ALU.add).then_inc(yb_ready, 1)

            pool.wait_ge(const_set, 1)
            with pool.Fori(0, TPC) as i:
                rstd_x(i)
                low_parts(i)
            for c in range(NCHUNK):
                if c == 1:
                    pool.wait_ge(result_out, 16)
                pre, post_ = pre_slots(c), post_slots(c)
                with pool.Fori(0, NQUAD) as i:
                    g_pre, g_post = TPC * (c + 1) + i, TPC * (c - 1) + i
                    pool.wait_ge(v_stored, TPC * (c + 1))
                    if pre:
                        rstd_x(g_pre)
                    for kb in range(periods[c]):
                        n = first_period[c] + i * periods[c] + kb
                        if c > 0:
                            pool.wait_ge(pv_done, n - 3)
                        pool.tensor_copy(v_ring[:, kb % 4], v_all[:, kb, bass.ds(i * QUAD, QUAD), :]
                                         ).then_inc(v_ready, 1)
                        if kb == 1 and post_:
                            gather_attention(g_post, c - 1, i)
                        if post_.get(kb - 1) == "o":
                            rstd_y(g_post)
                        if pre.get(kb) == "project":
                            low_parts(g_pre)
            with pool.Fori(0, TPC) as i:
                gather_attention(TILES - TPC + i, NCHUNK - 1, i)
                rstd_y(TILES - TPC + i)


def kernel(**inputs):
    import concourse.bacc as bacc
    from concourse.bass_utils import run_bass_kernel_spmd

    bf16 = mybir.dt.np(BF16) if hasattr(mybir.dt, "np") else None
    if bf16 is None:
        import ml_dtypes
        bf16 = ml_dtypes.bfloat16
    given = {name: np.asarray(a) for name, a in inputs.items()}

    def halves(w):
        return np.ascontiguousarray(w.reshape(KH, P, w.shape[1]).transpose(1, 0, 2))

    order = np.arange(D).reshape(H, KH, DK // KH).transpose(1, 2, 0).reshape(D)
    wq, wk, wv = (given[f"L0_attn_{n}_proj"] for n in "qkv")
    wo = given["L0_attn_o_proj"]
    o_rows = np.arange(D).reshape(2, 2, QUAD, DK).transpose(0, 2, 1, 3).reshape(D)
    lane = np.arange(P) % 32
    v_lane = np.stack([(lane // DK == q % 2) for q in range(NQUAD)], 1)
    second = np.broadcast_to(np.arange(NQUAD) % 2, (P, NQUAD))
    row = np.arange(P)
    tail = np.zeros((TAIL, H, CHUNK), np.float32)
    k_tail, q_tail = tail.copy(), tail.copy()
    k_tail[0:SHIFT_ROWS] = 1.0
    q_tail[0] = -SHIFT
    arrays = {
        "x": np.ascontiguousarray(given["L0_attn_in_features"].reshape(TILES, P, D).transpose(1, 0, 2)),
        "wqkv": halves(np.concatenate([wq[order].T, wk[order].T, wv.T], 1)),
        "wo": halves(np.ascontiguousarray(wo.T)[o_rows]),
        "wffn": halves(np.concatenate([given["L0_ffn_W"].T, given["L0_ffn_lora_A"].reshape(E * R, D).T,
                                       given["L0_ffn_gate_w"].T], 1)),
        "lora_b": np.ascontiguousarray(given["L0_ffn_lora_B"].transpose(0, 2, 1).reshape(E * R, D)),
        "biases": np.ascontiguousarray(np.broadcast_to(
            np.concatenate([given["L0_ffn_b"], given["L0_ffn_gate_b"]])[None], (P, D + E))),
        "ident": np.eye(P, dtype=np.float32),
        "ident_bf": np.eye(P, dtype=np.float32).astype(bf16),
        "masks": np.stack([np.where(row[None, :] >= row[:, None], BIG, 0.0),
                           np.where(row[None, :] <= row[:, None], BIG, -BIG)], 1).astype(np.float32),
        "lane_scales": np.stack([v_lane, 1.0 - v_lane, second], 1).astype(np.float32),
        "head_sum": (row[:, None] % H == np.arange(H)[None, :]).astype(np.float32).astype(bf16),
        "expert_ids": np.broadcast_to(np.arange(E, dtype=np.float32)[None], (P, E)).copy(),
        "k_tail": k_tail.astype(bf16),
        "q_tail": q_tail.astype(bf16),
    }
    nc = bacc.Bacc("TRN2", target_bir_lowering=False, num_devices=1)
    args = [nc.dram_tensor(n, a.shape, mybir.dt.from_np(a.dtype), kind="ExternalInput").ap()
            for n, a in arrays.items()]
    out = nc.dram_tensor("out", (TILES, P, D), F32, kind="ExternalOutput").ap()
    transformer_block(nc, *args, out)
    r = run_bass_kernel_spmd(nc, [arrays], core_ids=[0])
    return r.results[0]["out"].reshape(1, S, D)
```

```python
from contextlib import ExitStack

import numpy as np

import concourse.bass as bass
from concourse import mybir

F32 = mybir.dt.float32
BF16 = mybir.dt.bfloat16
I32 = mybir.dt.int32
U32 = mybir.dt.uint32
ALU = mybir.AluOpType
ACT = mybir.ActivationFunctionType
AX_X = mybir.AxisListType.X

P = 128
S, D = 2048, 256
H, DK = 16, 16
E, R = 8, 16
EPS = 1e-5
TILES = S // P
CHUNK = 512
NCHUNK = S // CHUNK
TPC = CHUNK // P
QUAD = 4
NQUAD = H // QUAD
KH = D // P
FFN = D + E * R + E

Q_SLOTS = (0, 0, 0, 1, 1, 1, 2)
K_SLOTS = (0, 1, 2, 0, 1, 2, 0)
K_RUNS = ((0, 2, 3), (6, 1, 1))
STACK = DK * len(Q_SLOTS)
SHIFT_ROWS = 3
TAIL = P - STACK

LAG = 2
V_RING = 4

BOUND, SHIFT = 40.0, 20.0
ROUNDING = 0.97
BIG = 3.0e38


def transformer_block(nc, x, wqkv, wo, wffn, lora_b, biases, ident, ident_bf, masks, head_sum,
                      expert_ids, k_tail, q_tail, out):
    ctx = ExitStack()
    with ctx:
        def sb(name, shape, dt=F32):
            return ctx.enter_context(nc.sbuf_tensor(name, shape, dt))

        def bank(name, shape, dt=F32):
            return ctx.enter_context(nc.psum_tensor(name, shape, dt))

        def sem(name):
            return ctx.enter_context(nc.semaphore(name))

        parts_dram = nc.dram_tensor("parts_dram", (NCHUNK, 2, 3, KH, P, CHUNK), BF16, kind="Internal").ap()
        shift_dram = nc.dram_tensor("shift_dram", (NCHUNK, H, SHIFT_ROWS * TPC, P), BF16, kind="Internal").ap()

        x_sb = sb("x_sb", [P, TILES, D])
        wqkv_sb = sb("wqkv_sb", [P, KH, 3 * D])
        wo_sb = sb("wo_sb", [P, KH, D])
        wffn_sb = sb("wffn_sb", [P, KH, FFN])
        lora_b_sb = sb("lora_b_sb", [P, D])
        biases_sb = sb("biases_sb", [P, D + E])
        ident_sb = sb("ident_sb", [P, P])
        ident_bf_sb = sb("ident_bf_sb", [P, P], BF16)
        masks_sb = sb("masks_sb", [P, 2, P])
        head_sum_sb = sb("head_sum_sb", [P, H], BF16)
        expert_ids_sb = sb("expert_ids_sb", [P, E])
        hold_cell = sb("hold_cell", [1, 1])
        minus_half = sb("minus_half", [P, TPC])
        k_stack = sb("k_stack", [P, NCHUNK, H, CHUNK], BF16)
        q_stack = sb("q_stack", [P, 2, H, CHUNK], BF16)
        v_all = sb("v_all", [P, TILES, H, DK])
        attn = sb("attn", [P, NQUAD, TPC, P])

        v_ring = sb("v_ring", [P, V_RING, QUAD, 32])
        probs = sb("probs", [P, LAG + 1, QUAD, CHUNK])
        bn1 = sb("bn1", [P, 6])
        mv1 = sb("mv1", [P, 2])
        ve1 = sb("ve1", [P, 1])
        rstd1 = sb("rstd1", [P, 1])
        xln = sb("xln", [P, D])
        xT = sb("xT", [P, KH, P])
        parts = sb("parts", [P, 2, 3, KH, P], BF16)
        rest1 = sb("rest1", [P, 2, KH, P])
        clamped = sb("clamped", [P, 2, KH, P], BF16)
        norms = sb("norms", [H, 2, TILES])
        first_bn = sb("first_bn", [P, TPC, 6])
        first_mv = sb("first_mv", [P, TPC, 2])
        first_ve = sb("first_ve", [P, TPC, 1])
        first_scale = sb("first_scale", [P, TPC])
        first_rest = probs[:, 0]
        first_xln = probs[:, 1, 0:2].rearrange("p a (b d) -> p (a b) d", d=D)
        first_xT = probs[:, 1, 2:4]
        slots = 2 * 3 * KH
        first_parts = q_stack[:, 1, 0:slots].rearrange("p (k s m) t -> p k s m t", k=2, s=3)
        first_squares = q_stack[:, 1, slots:slots + 2 * KH]
        norm_max = sb("norm_max", [H, 2])
        bound_sq = sb("bound_sq", [32, 32])
        bound_row = sb("bound_row", [32, 32])
        bound_max = sb("bound_max", [1, 1])
        is_bounded = sb("is_bounded", [1, NCHUNK], I32)
        row_max = sb("row_max", [P, 8])
        masked = sb("masked", [P, P])
        shift = sb("shift", [P, TPC])
        shift_rest = sb("shift_rest", [P, TPC])
        shift_parts = sb("shift_parts", [P, SHIFT_ROWS, TPC], BF16)
        shift_rows = sb("shift_rows", [SHIFT_ROWS * TPC, P], BF16)
        attn_in = sb("attn_in", [P, NQUAD, P])
        inverse = sb("inverse", [P, H])
        attn_y = sb("attn_y", [P, H, DK])
        attn_t = sb("attn_t", [P, KH, P])
        y = sb("y", [P, D])
        yb = sb("yb", [P, D])
        bn2 = sb("bn2", [P, 6])
        mv2 = sb("mv2", [P, 2])
        ve2 = sb("ve2", [P, 1])
        rstd2 = sb("rstd2", [P, 1])
        yln = sb("yln", [P, D])
        yT = sb("yT", [P, KH, P])
        logits = sb("logits", [P, E])
        top = sb("top", [P, 8])
        top_at = sb("top_at", [P, 8], U32)
        top_id = sb("top_id", [P, 2])
        top_gap = sb("top_gap", [P, 1])
        exp_gap = sb("exp_gap", [P, 1])
        gate_den = sb("gate_den", [P, 1])
        gate_of = sb("gate_of", [P, 2])
        gates2 = sb("gates2", [P, 2, E])
        gates = sb("gates", [P, E])
        gated = sb("gated", [P, E, R])
        gatedT = sb("gatedT", [P, P])
        result = sb("result", [P, D])

        scores = [bank(f"scores{a}", [P, 2, CHUNK]) for a in range(2)]
        acc = bank("acc", [P, CHUNK])
        pre_a = bank("pre_a", [P, 2, D])
        pre_b = bank("pre_b", [P, 2, KH, P])
        post = bank("post", [P, CHUNK])

        first_banks = [acc[:], post[:], pre_a[:].rearrange("p a d -> p (a d)"),
                       pre_b[:].rearrange("p k m t -> p (k m t)")]

        weights_in = sem("weights_in")
        x_in = [sem(f"x_in{c}") for c in range(NCHUNK)]
        x_rest_in = sem("x_rest_in")
        ident_in = sem("ident_in")
        consts_in = sem("consts_in")
        post_weights_in = sem("post_weights_in")
        tails_in = [sem(f"tails_in{par}") for par in range(2)]
        const_set = sem("const_set")
        ones_set = sem("ones_set")
        first_stats = sem("first_stats")
        first_scale_ready = sem("first_scale_ready")
        first_xln_ready = sem("first_xln_ready")
        first_xT_psum = sem("first_xT_psum")
        first_xT_ready = sem("first_xT_ready")
        first_qk_psum = sem("first_qk_psum")
        first_v_psum = sem("first_v_psum")
        first_v_stored = sem("first_v_stored")
        first_high = sem("first_high")
        first_rest_ready = sem("first_rest_ready")
        first_middle = sem("first_middle")
        first_low = sem("first_low")
        first_clamped = sem("first_clamped")
        first_squared = sem("first_squared")
        first_norm_psum = sem("first_norm_psum")
        first_k_out = sem("first_k_out")
        stats1 = sem("stats1")
        rstd1_ready = sem("rstd1_ready")
        xln_ready = sem("xln_ready")
        xT_psum = sem("xT_psum")
        xT_ready = sem("xT_ready")
        qk_psum = sem("qk_psum")
        v_psum = sem("v_psum")
        v_stored = sem("v_stored")
        split = sem("split")
        low_ready = sem("low_ready")
        norm_psum = sem("norm_psum")
        norm_read = sem("norm_read")
        parts_out = sem("parts_out")
        q_in = sem("q_in")
        k_in = sem("k_in")
        bound_step = sem("bound_step")
        gen_scores = [sem(f"gen_scores{c}") for c in range(NCHUNK)]
        gen_max = [sem(f"gen_max{c}") for c in range(NCHUNK)]
        gen_read = [sem(f"gen_read{c}") for c in range(NCHUNK)]
        gen_turned = [sem(f"gen_turned{c}") for c in range(NCHUNK)]
        gen_rows = [sem(f"gen_rows{c}") for c in range(NCHUNK)]
        gen_out = [sem(f"gen_out{c}") for c in range(NCHUNK)]
        gen_in = [sem(f"gen_in{c}") for c in range(NCHUNK)]
        scores_ready = sem("scores_ready")
        exp_done = sem("exp_done")
        causal_done = sem("causal_done")
        v_ready = sem("v_ready")
        pv_done = sem("pv_done")
        acc_read = sem("acc_read")
        attn_in_ready = sem("attn_in_ready")
        turned_psum = sem("turned_psum")
        inverse_ready = sem("inverse_ready")
        attn_y_ready = sem("attn_y_ready")
        attn_t_psum = sem("attn_t_psum")
        attn_t_ready = sem("attn_t_ready")
        o_psum = sem("o_psum")
        stats2 = sem("stats2")
        rstd2_ready = sem("rstd2_ready")
        yb_ready = sem("yb_ready")
        yln_ready = sem("yln_ready")
        yT_psum = sem("yT_psum")
        yT_ready = sem("yT_ready")
        ffn_psum = sem("ffn_psum")
        route = sem("route")
        gap_exp = sem("gap_exp")
        gatedT_psum = sem("gatedT_psum")
        gatedT_ready = sem("gatedT_ready")
        out_psum = sem("out_psum")
        result_ready = sem("result_ready")
        result_out = sem("result_out")

        STATS1, SPLIT, BOUND_STEPS, STATS2, ROUTE = 3, 5, 5, 4, 12
        Q_DMAS, K_DMAS = 3, 2

        periods = [TPC * (c + 1) for c in range(NCHUNK)]
        first_period = [NQUAD * sum(periods[:c]) for c in range(NCHUNK)]

        def span(c, kb):
            return max(0, kb - TPC * c) * P

        PRE_SLOTS = ({1: ["turn"], 2: ["project"], 4: ["norm"]}, {1: ["turn"], 4: ["project"], 6: ["norm"]},
                     {1: ["turn"], 4: ["project"], 6: ["norm"]}, {})
        POST_SLOTS = ({}, *({0: ["turn_sums"], 1: ["turn_back"], 3: ["o"], 5: ["turn"], 6: ["ffn"],
                             8: ["turn_gated"], 9: ["lora"]},) * 3)

        def sums_of_quad(c, i):
            return attn[:, bass.ds(i, 1), :, :] if c % 2 == 0 else attn[:, :, bass.ds(i, 1), :]

        def sums_of_tile(c, i):
            return attn[:, :, bass.ds(i, 1), :] if c % 2 == 0 else attn[:, bass.ds(i, 1), :, :]

        block = ctx.enter_context(nc.Block())

        @block.sync
        def _(sp):
            sp.dma_start(x_sb[:, 0:2, :], x[:, 0:2, :]).then_inc(x_in[0], 16)
            sp.dma_start(x_sb[:, 2:TPC, :], x[:, 2:TPC, :]).then_inc(x_rest_in, 16)
            sp.dma_start(ident_sb[:], ident).then_inc(ident_in, 16)
            sp.dma_start(wqkv_sb[:], wqkv).then_inc(weights_in, 16)
            sp.dma_start(head_sum_sb[:], head_sum).then_inc(consts_in, 16)
            sp.dma_start(masks_sb[:], masks).then_inc(consts_in, 16)
            sp.dma_start(ident_bf_sb[:], ident_bf).then_inc(consts_in, 16)
            sp.dma_start(q_stack[STACK:P, 0], q_tail).then_inc(tails_in[0], 16)
            for c in range(NCHUNK):
                sp.dma_start(k_stack[STACK:P, c], k_tail).then_inc(tails_in[0], 16)
            sp.dma_start(x_sb[:, TPC:2 * TPC, :], x[:, TPC:2 * TPC, :]).then_inc(x_in[1], 16)

            def load_rest():
                for c in range(2, NCHUNK):
                    sp.dma_start(x_sb[:, c * TPC:(c + 1) * TPC, :], x[:, c * TPC:(c + 1) * TPC, :]
                                 ).then_inc(x_in[c], 16)
                sp.dma_start(wo_sb[:], wo).then_inc(post_weights_in, 16)
                sp.dma_start(wffn_sb[:], wffn).then_inc(post_weights_in, 16)
                sp.dma_start(lora_b_sb[:], lora_b).then_inc(post_weights_in, 16)
                sp.dma_start(biases_sb[:], biases).then_inc(result_out, 16)
                sp.dma_start(expert_ids_sb[:], expert_ids).then_inc(post_weights_in, 16)

            def store_parts(c, i):
                u = (c - 1) * TPC + i
                sp.wait_ge(low_ready, u + 1)
                sp.wait_ge(split, SPLIT * u + 4)
                sp.dma_start(parts_dram[c, :, :, :, :, bass.ds(i * P, P)].rearrange("k s m p t -> p (k s m) t"),
                             parts[:].rearrange("p k s m t -> p (k s m) t")).then_inc(parts_out, 16)

            def part_rows(c, k, heads):
                return parts_dram[c, k].rearrange("s m (d h) t -> (s m d) h t", h=H)[:, heads, :]

            def load_stacks(c, quad):
                first = c == 0 and isinstance(quad, int)
                heads = bass.ds(quad * QUAD if isinstance(quad, int) else sp.snap(quad * QUAD), QUAD)
                if first:
                    sp.wait_ge(parts_out, 16)
                else:
                    sp.wait_ge(q_in, 16 * Q_DMAS * (NQUAD * c + quad))
                rows = part_rows(c, 0, heads)
                for part in range(3):
                    first_slot, n = Q_SLOTS.index(part), Q_SLOTS.count(part)
                    sp.dma_start(q_stack[first_slot * DK:(first_slot + n) * DK, c % 2, heads, :],
                                 rows[part * DK:(part + 1) * DK].unsqueeze(0).to_broadcast([n, DK, QUAD, CHUNK])
                                 ).then_inc(q_in, 16)
                if first:
                    sp.wait_ge(first_k_out, 16)
                else:
                    sp.wait_ge(k_in, 16 * K_DMAS * (NQUAD * c + quad))
                rows = part_rows(c, 1, heads)
                for first_slot, n, k in K_RUNS:
                    sp.dma_start(k_stack[first_slot * DK:(first_slot + n * k) * DK, c, heads, :],
                                 rows[0:k * DK].unsqueeze(0).to_broadcast([n, k * DK, QUAD, CHUNK])
                                 ).then_inc(k_in, 16)

            def store_shifts(c):
                sp.wait_ge(q_in, 16 * Q_DMAS * NQUAD * (c + 1))
                sp.wait_ge(tails_in[c % 2], 16 * (1 if c % 2 else 1 + NCHUNK))
                with sp.Fori(0, H) as h:
                    sp.wait_ge(gen_rows[c], h + 1)
                    sp.dma_start(shift_dram[c, h], shift_rows[:]).then_inc(gen_out[c], 16)
                    sp.wait_ge(gen_out[c], 16 * (h + 1))
                    sp.dma_start(q_stack[STACK:STACK + SHIFT_ROWS, c % 2, h, :],
                                 shift_dram[c, h].rearrange("(s i) t -> s (i t)", s=SHIFT_ROWS)
                                 ).then_inc(gen_in[c], 16)

            for k in range(2):
                sp.wait_ge(first_low, KH * (k + 1))
                sp.dma_start(parts_dram[0, k].rearrange("s m p t -> p (s m) t"),
                             first_parts[:, k].rearrange("p s m t -> p (s m) t")
                             ).then_inc(first_k_out if k else parts_out, 16)
            for c in range(NCHUNK):
                if c > 0:
                    sp.wait_ge(parts_out, 16 * (1 + TPC * c))
                load_stacks(c, 0)
                sp.wait_ge(bound_step, BOUND_STEPS * (c + 1))
                if c == 0:
                    sp.dma_start(q_stack[STACK:P, 1], q_tail).then_inc(tails_in[1], 16)
                    load_rest()
                bounded = sp.value_load(is_bounded[0:1, c:c + 1], min_val=0, max_val=1)
                with sp.If(bounded == 0):
                    with sp.Fori(1, NQUAD) as quad:
                        load_stacks(c, quad)
                    store_shifts(c)
                    if c + 1 < NCHUNK:
                        with sp.Fori(0, TPC) as i:
                            store_parts(c + 1, i)
                with sp.If(bounded == 1):
                    with sp.Fori(1, NQUAD) as quad:
                        load_stacks(c, quad)
                        if c + 1 < NCHUNK:
                            store_parts(c + 1, quad - 1)
                    if c + 1 < NCHUNK:
                        store_parts(c + 1, TPC - 1)
            sp.wait_ge(parts_out, 16 * (1 + TILES - TPC))
            sp.wait_ge(result_out, 16 * (TILES + 1))

        @block.tensor
        def _(pe):
            def project_first_chunk():
                pe.wait_ge(ident_in, 16)
                for t in range(TPC):
                    pe.wait_ge(first_xln_ready, t + 1)
                    for k in range(KH):
                        m = pe.transpose(scores[t // 2][:, t % 2, k * P:(k + 1) * P],
                                         first_xln[:, t, k * P:(k + 1) * P], ident_sb[:])
                    m.then_inc(first_xT_psum, 1)
                pe.wait_ge(weights_in, 16)
                pe.wait_ge(const_set, 1)
                pe.wait_ge(first_xT_ready, TPC)
                for n in range(2 * KH):
                    for k in range(KH):
                        m = pe.matmul(first_banks[n], wqkv_sb[:, k, n * P:(n + 1) * P], first_xT[:, k, :],
                                      start=(k == 0), stop=(k == KH - 1))
                    m.then_inc(first_qk_psum, 1)
                for t in range(TPC):
                    for k in range(KH):
                        m = pe.matmul(scores[t // 2][:, t % 2, 0:D], first_xT[:, k, t * P:(t + 1) * P],
                                      wqkv_sb[:, k, 2 * D:3 * D], start=(k == 0), stop=(k == KH - 1))
                    m.then_inc(first_v_psum, 1)
                pe.wait_ge(consts_in, 16 * 3)
                pe.wait_ge(first_squared, 2 * KH)
                for a in range(2):
                    for k in range(KH):
                        m = pe.matmul(first_banks[a][0:H], head_sum_sb[:], first_squares[:, a * KH + k, :],
                                      start=(k == 0), stop=(k == KH - 1))
                    m.then_inc(first_norm_psum, 1)
                pe.wait_ge(first_v_stored, TPC)

            def turn_x(g):
                pe.wait_ge(xln_ready, g - TPC + 1)
                for k in range(KH):
                    t = pe.transpose(pre_a[:, 0, k * P:(k + 1) * P], xln[:, k * P:(k + 1) * P], ident_sb[:])
                t.then_inc(xT_psum, 1)

            def project(g):
                pe.wait_ge(xT_ready, g - TPC + 1)
                for n in range(2 * KH):
                    for k in range(KH):
                        m = pe.matmul(pre_b[:, n // KH, n % KH, :], wqkv_sb[:, k, n * P:(n + 1) * P], xT[:, k, :],
                                      start=(k == 0), stop=(k == KH - 1))
                m.then_inc(qk_psum, 1)
                for k in range(KH):
                    m = pe.matmul(pre_a[:, 1, :], xT[:, k, :], wqkv_sb[:, k, 2 * D:3 * D],
                                  start=(k == 0), stop=(k == KH - 1))
                m.then_inc(v_psum, 1)

            def sum_squares(g):
                pe.wait_ge(split, SPLIT * (g - TPC + 1))
                for k in range(KH):
                    m = pe.matmul(pre_b[0:H, :, 0, :], head_sum_sb[:], clamped[:, :, k, :],
                                  start=(k == 0), stop=(k == KH - 1))
                m.then_inc(norm_psum, 1)

            PRE = {"turn": turn_x, "project": project, "norm": sum_squares}

            def turn_sums(g):
                pe.wait_ge(attn_in_ready, g + 1)
                pe.wait_ge(result_ready, g + 1)
                for q in range(NQUAD):
                    t = pe.transpose(post[:, q * P:(q + 1) * P], attn_in[:, q, :], ident_sb[:])
                t.then_inc(turned_psum, 1)

            def turn_back(g):
                pe.wait_ge(attn_y_ready, g + 1)
                for k in range(KH):
                    t = pe.transpose(post[:, k * P:(k + 1) * P],
                                     attn_y[:].rearrange("p h d -> p (h d)")[:, k * P:(k + 1) * P], ident_sb[:])
                t.then_inc(attn_t_psum, 1)

            def o_proj(g):
                pe.wait_ge(attn_t_ready, g + 1)
                for k in range(KH):
                    m = pe.matmul(post[:, 0:D], attn_t[:, k, :], wo_sb[:, k, :], start=(k == 0), stop=(k == KH - 1))
                m.then_inc(o_psum, 1)

            def turn_y(g):
                pe.wait_ge(yln_ready, g + 1)
                for k in range(KH):
                    t = pe.transpose(post[:, D + k * P:D + (k + 1) * P], yln[:, k * P:(k + 1) * P], ident_sb[:])
                t.then_inc(yT_psum, 1)

            def ffn(g):
                pe.wait_ge(yT_ready, g + 1)
                for k in range(KH):
                    m = pe.matmul(post[:, 0:FFN], yT[:, k, :], wffn_sb[:, k, :], start=(k == 0), stop=(k == KH - 1),
                                  skip_group_check=True)
                m.then_inc(ffn_psum, 1)

            def turn_gated(g):
                pe.wait_ge(route, ROUTE * (g + 1))
                pe.transpose(pre_a[:, 0, 0:P], gated[:].rearrange("p e r -> p (e r)"), ident_sb[:]
                             ).then_inc(gatedT_psum, 1)

            def lora(g):
                pe.wait_ge(gatedT_ready, g + 1)
                pe.matmul(post[:, 0:D], gatedT[:], lora_b_sb[:], start=False, stop=True,
                          skip_group_check=True).then_inc(out_psum, 1)

            POST = {"turn_sums": turn_sums, "turn_back": turn_back, "o": o_proj, "turn": turn_y, "ffn": ffn,
                    "turn_gated": turn_gated, "lora": lora}

            def row_maxima(c):
                with pe.Fori(0, H) as h:
                    for i in range(TPC):
                        if i > 0:
                            pe.wait_ge(gen_read[c], TPC * h + i)
                        lhs = q_stack[0:STACK, c % 2, h, i * P:(i + 1) * P]
                        for kc in range(c + 1):
                            n = CHUNK if kc < c else (i + 1) * P
                            m = pe.matmul(scores[kc // 2][:, kc % 2, 0:n], lhs,
                                          k_stack[0:STACK, kc, h, 0:n], start=True, stop=True)
                        m.then_inc(gen_scores[c], 1)
                    pe.wait_ge(gen_max[c], h + 1)
                    pe.transpose(post[0:SHIFT_ROWS * TPC, 0:P // 2].bitcast(BF16),
                                 shift_parts[:].rearrange("p s i -> p (s i)"), ident_bf_sb[:]
                                 ).then_inc(gen_turned[c], 1)
                pe.wait_ge(gen_in[c], 16 * H)

            def attend(c, i):
                last = periods[c] - 1
                base = first_period[c] + i * periods[c]
                quad_no = NQUAD * c + i

                def qk(kb):
                    n, lo = base + kb, span(c, kb)
                    if kb == TPC * c:
                        pe.wait_ge(k_in, 16 * K_DMAS * (quad_no + 1))
                    for a in range(2):
                        if kb > 0:
                            pe.wait_ge(exp_done, 2 * n + a - 1)
                        for j in range(2):
                            head = i * QUAD + 2 * a + j
                            m = pe.matmul(scores[a][:, j, lo:CHUNK], k_stack[:, kb // TPC, head, kb % TPC * P:(kb % TPC + 1) * P],
                                          q_stack[:, c % 2, head, lo:CHUNK], start=True, stop=True)
                        m.then_inc(scores_ready, 1)

                def pv(kb):
                    n, lo = base + kb, span(c, kb)
                    pe.wait_ge(exp_done, 2 * n + 2)
                    pe.wait_ge(v_ready, n + 1)
                    if kb >= TPC * c:
                        pe.wait_ge(causal_done, TPC * quad_no + kb - TPC * c + 1)
                    if kb == 0:
                        pe.wait_ge(acc_read, quad_no + 1)
                    for j in range(QUAD):
                        m = pe.matmul(acc[32 * j:32 * j + 32, lo:CHUNK], v_ring[:, kb % V_RING, j, :],
                                      probs[:, kb % (LAG + 1), j, lo:CHUNK], start=(kb == 0), stop=(kb == last),
                                      tile_position=(0, 32 * j))
                    m.then_inc(pv_done, 1)

                for k in range(periods[c] + LAG):
                    if k < periods[c]:
                        qk(k)
                    for name in PRE_SLOTS[c].get(k, ()):
                        PRE[name](TPC * (c + 1) + i)
                    for name in POST_SLOTS[c].get(k, ()):
                        POST[name](TPC * (c - 1) + i)
                    if k >= LAG:
                        pv(k - LAG)

            project_first_chunk()
            for c in range(NCHUNK):
                if c < 2:
                    pe.wait_ge(tails_in[c], 16 * (1 if c else 1 + NCHUNK))
                pe.wait_ge(bound_step, BOUND_STEPS * (c + 1))
                bounded = pe.value_load(is_bounded[0:1, c:c + 1], min_val=0, max_val=1)
                with pe.If(bounded == 0):
                    pe.wait_ge(q_in, 16 * Q_DMAS * NQUAD * (c + 1))
                    pe.wait_ge(k_in, 16 * K_DMAS * NQUAD * (c + 1))
                    if c > 0:
                        pe.wait_ge(exp_done, 2 * first_period[c])
                    row_maxima(c)
                if c == 1:
                    pe.wait_ge(post_weights_in, 16 * 4)
                with pe.Fori(0, NQUAD) as i:
                    pe.wait_ge(q_in, 16 * Q_DMAS * (NQUAD * c + i + 1))
                    attend(c, i)
            with pe.Fori(0, TPC) as i:
                for name in POST:
                    POST[name](TILES - TPC + i)

        @block.scalar
        def _(act):
            def exp_gap_of(g):
                act.wait_ge(route, ROUTE * g + 4)
                act.activation(exp_gap[:], top_gap[:], ACT.Exp).then_inc(gap_exp, 1)

            def store(g):
                act.wait_ge(result_ready, g + 2)
                act.dma_start(out[g], result[:]).then_inc(result_out, 16)

            for t in range(TPC):
                act.wait_ge(first_xT_psum, t + 1)
                act.copy(first_xT[:, :, t * P:(t + 1) * P],
                         scores[t // 2][:, t % 2, 0:D].rearrange("p (k t) -> p k t", k=KH)
                         ).then_inc(first_xT_ready, 1)
            for n in range(2 * KH + 1):
                if n < 2 * KH:
                    act.wait_ge(first_qk_psum, n + 1)
                    act.copy(first_parts[:, n // KH, 0, n % KH, :], first_banks[n]).then_inc(first_high, 1)
                if n > 0:
                    act.wait_ge(first_rest_ready, n)
                    act.copy(first_parts[:, (n - 1) // KH, 1, (n - 1) % KH, :], first_rest[:, n - 1]
                             ).then_inc(first_middle, 1)
            for t in range(TPC):
                act.wait_ge(first_v_psum, t + 1)
                act.copy(v_all[:, t].rearrange("p h d -> p (h d)"), scores[t // 2][:, t % 2, 0:D]
                         ).then_inc(first_v_stored, 1)

            for c in range(NCHUNK):
                with act.Fori(0, NQUAD) as i:
                    base = first_period[c] + i * periods[c]
                    for kb in range(periods[c]):
                        n, lo = base + kb, span(c, kb)
                        for a in range(2):
                            act.wait_ge(scores_ready, 2 * n + a + 1)
                            act.activation(probs[:, kb % (LAG + 1), 2 * a:2 * a + 2, lo:CHUNK], scores[a][:, :, lo:CHUNK],
                                           ACT.Exp).then_inc(exp_done, 1)
                        if "ffn" in POST_SLOTS[c].get(kb - 1, ()):
                            exp_gap_of(TPC * (c - 1) + i)
                    if c > 0:
                        store(TPC * (c - 1) + i)
            with act.Fori(0, TPC) as i:
                exp_gap_of(TILES - TPC + i)
                store(TILES - TPC + i)

        @block.vector
        def _(dve):
            dve.memset(minus_half[:], -0.5).then_inc(acc_read, 1)
            dve.memset(bound_sq[:], 0.0).then_inc(result_ready, 1)
            def hold_here():
                dve.memset(hold_cell[:], 0.0)

            def project_first_chunk():
                for t in range(TPC):
                    if t % 2 == 0:
                        dve.wait_ge(x_rest_in if t else x_in[0], 16)
                    dve.bn_stats(first_bn[:, t, :], x_sb[:, t, :]).then_inc(first_stats, 1)
                for t in range(TPC):
                    dve.wait_ge(first_stats, TPC)
                    dve.bn_aggr(first_mv[:, t, :], first_bn[:, t, :]).then_inc(first_stats, 1)
                dve.wait_ge(first_stats, 2 * TPC)
                dve.tensor_scalar(first_ve[:], first_mv[:, :, 1:2], EPS, None, ALU.add).then_inc(first_stats, 1)
                dve.wait_ge(first_scale_ready, 1)
                for t in range(TPC):
                    dve.tensor_scalar(first_xln[:, t, :], x_sb[:, t, :], first_mv[:, t, 0:1], first_scale[:, t:t + 1],
                                      ALU.subtract, ALU.mult).then_inc(first_xln_ready, 1)
                dve.wait_ge(weights_in, 16)
                dve.tensor_scalar(wqkv_sb[:, :, 0:D], wqkv_sb[:, :, 0:D], float(DK) ** -0.5, None,
                                  ALU.mult).then_inc(const_set, 1)
                for n in range(2 * KH + 1):
                    if n < 2 * KH:
                        dve.wait_ge(first_high, n + 1)
                        dve.tensor_tensor(first_rest[:, n], first_banks[n], first_parts[:, n // KH, 0, n % KH, :],
                                          ALU.subtract).then_inc(first_rest_ready, 1)
                    if n > 0:
                        dve.wait_ge(first_middle, n)
                        dve.tensor_tensor(first_parts[:, (n - 1) // KH, 2, (n - 1) % KH, :], first_rest[:, n - 1],
                                          first_parts[:, (n - 1) // KH, 1, (n - 1) % KH, :],
                                          ALU.subtract).then_inc(first_low, 1)
                for n in range(2 * KH):
                    dve.tensor_scalar(first_squares[:, n], first_parts[:, n // KH, 0, n % KH, :], 1e15, -1e15,
                                      ALU.min, ALU.max).then_inc(first_clamped, 1)
                for n in range(2 * KH):
                    dve.wait_ge(first_clamped, n + 1)
                    dve.tensor_tensor(first_squares[:, n], first_squares[:, n], first_squares[:, n],
                                      ALU.mult).then_inc(first_squared, 1)
                for a in range(2):
                    dve.wait_ge(first_norm_psum, a + 1)
                    dve.tensor_reduce(norms[:, a, 0:TPC], first_banks[a][0:H].rearrange("h (i t) -> h i t", i=TPC),
                                      AX_X, ALU.max).then_inc(norm_read, 1)

            def normalise_x(g):
                dve.bn_stats(bn1[:], x_sb[:, g, :]).then_inc(stats1, 1)
                dve.wait_ge(stats1, STATS1 * (g - TPC) + 1)
                hold_here()
                dve.bn_aggr(mv1[:], bn1[:]).then_inc(stats1, 1)
                dve.wait_ge(stats1, STATS1 * (g - TPC) + 2)
                dve.tensor_scalar(ve1[:], mv1[:, 1:2], EPS, None, ALU.add).then_inc(stats1, 1)
                dve.wait_ge(rstd1_ready, g - TPC + 1)
                dve.tensor_scalar(xln[:], x_sb[:, g, :], mv1[:, 0:1], rstd1[:], ALU.subtract,
                                  ALU.mult).then_inc(xln_ready, 1)

            def store_xT(g):
                dve.wait_ge(xT_psum, g - TPC + 1)
                dve.tensor_copy(xT[:].rearrange("p k t -> p (k t)"), pre_a[:, 0, :]).then_inc(xT_ready, 1)

            def split_qk(g):
                base = SPLIT * (g - TPC)
                dve.wait_ge(qk_psum, g - TPC + 1)
                dve.wait_ge(parts_out, 16 * (g - TPC + 1))
                high, middle = parts[:, :, 0], parts[:, :, 1]
                dve.tensor_copy(high, pre_b[:]).then_inc(split, 1)
                dve.wait_ge(split, base + 1)
                dve.tensor_tensor(rest1[:], pre_b[:], high, ALU.subtract).then_inc(split, 1)
                dve.tensor_scalar(clamped[:], high, 1e15, -1e15, ALU.min, ALU.max).then_inc(split, 1)
                dve.wait_ge(split, base + 3)
                dve.tensor_copy(middle, rest1[:]).then_inc(split, 1)
                dve.tensor_tensor(clamped[:], clamped[:], clamped[:], ALU.mult).then_inc(split, 1)

            def store_v(g):
                dve.wait_ge(v_psum, g - TPC + 1)
                dve.tensor_copy(v_all[:, g].rearrange("p h d -> p (h d)"), pre_a[:, 1, :]).then_inc(v_stored, 1)

            def read_norms(g):
                dve.wait_ge(norm_psum, g - TPC + 1)
                dve.tensor_reduce(norms[:, :, bass.ds(g, 1)], pre_b[0:H, :, 0, :], AX_X, ALU.max).then_inc(norm_read, 1)

            def decide_bound(c):
                base = BOUND_STEPS * c
                dve.wait_ge(norm_read, 2 + TPC * c)
                dve.tensor_reduce(norm_max[:], norms[:, :, 0:TPC * (c + 1)], AX_X, ALU.max).then_inc(bound_step, 1)
                dve.wait_ge(bound_step, base + 1)
                dve.tensor_scalar(bound_sq[0:H, 0:1], norm_max[:, 0:1], norm_max[:, 1:2], None,
                                  ALU.mult).then_inc(bound_step, 1)
                dve.wait_ge(bound_step, base + 2)
                dve.transpose(bound_row[:], bound_sq[:]).then_inc(bound_step, 1)
                dve.wait_ge(bound_step, base + 3)
                dve.tensor_reduce(bound_max[:], bound_row[0:1, 0:H], AX_X, ALU.max).then_inc(bound_step, 1)
                dve.wait_ge(bound_step, base + 4)
                dve.tensor_scalar(is_bounded[:, c:c + 1], bound_max[:], BOUND * BOUND * ROUNDING, None,
                                  ALU.is_le).then_inc(bound_step, 1)
                dve.wait_ge(bound_step, base + 5)

            def shifts(c):
                step = 0
                with dve.Fori(0, H) as h:
                    for i in range(TPC):
                        done = h * (TPC * GEN_STEPS + GEN_SPLIT) + i * GEN_STEPS
                        step = gen_step[c]
                        dve.memset(row_max[:], -BIG).then_inc(step, 1)
                        dve.wait_ge(gen_scores[c], TPC * h + i + 1)
                        dve.wait_ge(step, done + 1)
                        dve.tensor_tensor(masked[:], scores[c // 2][:, c % 2, i * P:(i + 1) * P], masks_sb[:, 1, :],
                                          ALU.min).then_inc(step, 1)
                        for kc in range(c):
                            dve.tensor_reduce(row_max[:, kc:kc + 1], scores[kc // 2][:, kc % 2, :], AX_X, ALU.max)
                        if i > 0:
                            dve.tensor_reduce(row_max[:, 4:5], scores[c // 2][:, c % 2, 0:i * P], AX_X, ALU.max)
                        dve.wait_ge(step, done + 2)
                        dve.tensor_reduce(row_max[:, 5:6], masked[:], AX_X, ALU.max).then_inc(gen_read[c], 1)
                        dve.wait_ge(gen_read[c], TPC * h + i + 1)
                        dve.tensor_reduce(masked[:, 0:1], row_max[:], AX_X, ALU.max).then_inc(step, 1)
                        dve.wait_ge(step, done + 3)
                        dve.tensor_scalar(shift[:, i:i + 1], masked[:, 0:1], -1.0, None, ALU.mult).then_inc(step, 1)
                    done = h * (TPC * GEN_STEPS + GEN_SPLIT) + TPC * GEN_STEPS
                    dve.wait_ge(step, done)
                    dve.tensor_copy(shift_parts[:, 0], shift[:]).then_inc(step, 1)
                    dve.wait_ge(step, done + 1)
                    dve.tensor_tensor(shift_rest[:], shift[:], shift_parts[:, 0], ALU.subtract).then_inc(step, 1)
                    dve.wait_ge(step, done + 2)
                    dve.tensor_copy(shift_parts[:, 1], shift_rest[:]).then_inc(step, 1)
                    dve.wait_ge(step, done + 3)
                    dve.tensor_tensor(shift_parts[:, 2], shift_rest[:], shift_parts[:, 1],
                                      ALU.subtract).then_inc(gen_max[c], 1)
                    dve.wait_ge(gen_turned[c], h + 1)
                    dve.tensor_copy(shift_rows[:], post[0:SHIFT_ROWS * TPC, 0:P // 2].bitcast(BF16)
                                    ).then_inc(gen_rows[c], 1)
                    dve.wait_ge(gen_out[c], 16 * (h + 1))

            def clear_later_keys(c, i, kb):
                n, j = first_period[c] + i * periods[c] + kb, kb - TPC * c
                dve.wait_ge(exp_done, 2 * n + 2)
                tile = probs[:, kb % (LAG + 1), :, j * P:(j + 1) * P]
                mask = masks_sb[:, 0:1, :].to_broadcast([P, QUAD, P])
                dve.tensor_tensor(tile, tile, mask, ALU.min).then_inc(causal_done, 1)

            def keep_sums(c, i):
                dve.wait_ge(pv_done, first_period[c] + (i + 1) * periods[c])
                dve.tensor_copy(sums_of_quad(c, i), acc[:].rearrange("p (a t) -> p a t", a=TPC).unsqueeze(
                    1 if c % 2 == 0 else 2)).then_inc(acc_read, 1)

            def divide(g):
                turned = post[:].rearrange("p (h d) -> p h d", d=32)
                dve.wait_ge(turned_psum, g + 1)
                dve.reciprocal(inverse[:].unsqueeze(2), turned[:, :, DK:DK + 1]).then_inc(inverse_ready, 1)
                dve.wait_ge(inverse_ready, g + 1)
                dve.tensor_tensor(attn_y[:], turned[:, :, 0:DK], inverse[:].unsqueeze(2).to_broadcast([P, H, DK]),
                                  ALU.mult).then_inc(attn_y_ready, 1)

            def store_attn_t(g):
                dve.wait_ge(attn_t_psum, g + 1)
                dve.tensor_copy(attn_t[:].rearrange("p k t -> p (k t)"), post[:, 0:D]).then_inc(attn_t_ready, 1)

            def residual_and_stats(g):
                base = STATS2 * g
                dve.wait_ge(o_psum, g + 1)
                dve.tensor_tensor(y[:], post[:, 0:D], x_sb[:, g, :], ALU.add).then_inc(stats2, 1)
                dve.wait_ge(stats2, base + 1)
                dve.bn_stats(bn2[:], y[:]).then_inc(stats2, 1)
                dve.wait_ge(stats2, base + 2)
                hold_here()
                dve.bn_aggr(mv2[:], bn2[:]).then_inc(stats2, 1)
                dve.wait_ge(stats2, base + 3)
                dve.tensor_scalar(ve2[:], mv2[:, 1:2], EPS, None, ALU.add).then_inc(stats2, 1)
                dve.wait_ge(rstd2_ready, g + 1)
                dve.tensor_scalar(yln[:], y[:], mv2[:, 0:1], rstd2[:], ALU.subtract, ALU.mult).then_inc(yln_ready, 1)

            def store_yT(g):
                dve.wait_ge(yT_psum, g + 1)
                dve.tensor_copy(yT[:].rearrange("p k t -> p (k t)"), post[:, D:2 * D]).then_inc(yT_ready, 1)

            def route_tokens(g):
                base = ROUTE * g
                dve.wait_ge(result_out, 16)
                dve.wait_ge(ffn_psum, g + 1)
                dve.tensor_tensor(logits[:], post[:, D + E * R:FFN], biases_sb[:, D:D + E], ALU.add).then_inc(route, 1)
                dve.wait_ge(route, base + 1)
                hold_here()
                dve.max(top[:], logits[:]).then_inc(route, 1)
                dve.wait_ge(route, base + 2)
                hold_here()
                dve.max_index(top_at[:], top[:], logits[:]).then_inc(route, 1)
                dve.tensor_scalar(top_gap[:], top[:, 1:2], top[:, 0:1], None, ALU.subtract).then_inc(route, 1)
                dve.wait_ge(route, base + 3)
                dve.tensor_copy(top_id[:], top_at[:, 0:2]).then_inc(route, 1)
                dve.wait_ge(gap_exp, g + 1)
                dve.tensor_scalar(gate_den[:], exp_gap[:], 1.0, None, ALU.add).then_inc(route, 1)
                dve.wait_ge(route, base + 6)
                dve.reciprocal(gate_of[:, 0:1], gate_den[:]).then_inc(route, 1)
                dve.wait_ge(route, base + 7)
                dve.tensor_scalar(gate_of[:, 1:2], gate_of[:, 0:1], exp_gap[:], None, ALU.mult).then_inc(route, 1)
                dve.wait_ge(route, base + 8)
                for n in range(2):
                    dve.tensor_scalar(gates2[:, n, :], expert_ids_sb[:], top_id[:, n:n + 1], gate_of[:, n:n + 1],
                                      ALU.is_equal, ALU.mult).then_inc(route, 1)
                dve.wait_ge(route, base + 10)
                dve.tensor_tensor(gates[:], gates2[:, 0, :], gates2[:, 1, :], ALU.add).then_inc(route, 1)
                dve.wait_ge(route, base + 11)
                dve.tensor_tensor(gated[:], post[:, D:D + E * R].rearrange("p (e r) -> p e r", e=E),
                                  gates[:].unsqueeze(2).to_broadcast([P, E, R]), ALU.mult).then_inc(route, 1)

            def store_gatedT(g):
                dve.wait_ge(gatedT_psum, g + 1)
                dve.tensor_copy(gatedT[:], pre_a[:, 0, 0:P]).then_inc(gatedT_ready, 1)

            def finish(g):
                dve.wait_ge(out_psum, g + 1)
                dve.wait_ge(yb_ready, g + 1)
                dve.wait_ge(result_out, 16 * (g + 1))
                dve.tensor_tensor(result[:], post[:, 0:D], yb[:], ALU.add).then_inc(result_ready, 1)

            POST = {"turn_sums": divide, "turn_back": store_attn_t, "o": residual_and_stats, "turn": store_yT,
                    "ffn": route_tokens, "turn_gated": store_gatedT, "lora": finish}

            def project_out(g):
                split_qk(g)
                store_v(g)

            PRE = {"turn": store_xT, "project": project_out, "norm": read_norms}

            GEN_STEPS, GEN_SPLIT = 4, 3
            gen_step = [sem(f"gen_step{c}") for c in range(NCHUNK)]

            project_first_chunk()
            for c in range(NCHUNK):
                decide_bound(c)
                bounded = dve.value_load(is_bounded[0:1, c:c + 1], min_val=0, max_val=1)
                with dve.If(bounded == 0):
                    shifts(c)
                if c + 1 < NCHUNK:
                    dve.wait_ge(x_in[c + 1], 16)
                if c == 1:
                    dve.wait_ge(post_weights_in, 16 * 4)
                with dve.Fori(0, NQUAD) as i:
                    if PRE_SLOTS[c]:
                        normalise_x(TPC * (c + 1) + i)
                    for k in range(periods[c] + LAG):
                        if TPC * c < k <= periods[c]:
                            clear_later_keys(c, i, k - 1)
                        for name in PRE_SLOTS[c].get(k, ()):
                            PRE[name](TPC * (c + 1) + i)
                        for name in POST_SLOTS[c].get(k, ()):
                            POST[name](TPC * (c - 1) + i)
                    keep_sums(c, i)
            with dve.Fori(0, TPC) as i:
                for name in POST:
                    POST[name](TILES - TPC + i)

        @block.gpsimd
        def _(pool):
            def rstd_x(g):
                pool.wait_ge(stats1, STATS1 * (g - TPC + 1))
                pool.tensor_tensor(rstd1[:], ve1[:], minus_half[:, 0:1], ALU.pow).then_inc(rstd1_ready, 1)

            def low_parts(g):
                pool.wait_ge(split, SPLIT * (g - TPC) + 4)
                pool.tensor_tensor(parts[:, :, 2], rest1[:], parts[:, :, 1], ALU.subtract).then_inc(low_ready, 1)

            def gather_sums(g, c, i):
                pool.wait_ge(acc_read, NQUAD * (c + 1) + 1)
                pool.tensor_copy(attn_in[:].unsqueeze(2 if c % 2 == 0 else 1), sums_of_tile(c, i)
                                 ).then_inc(attn_in_ready, 1)

            def rstd_y(g):
                pool.wait_ge(stats2, STATS2 * (g + 1))
                pool.tensor_tensor(rstd2[:], ve2[:], minus_half[:, 0:1], ALU.pow).then_inc(rstd2_ready, 1)
                pool.tensor_tensor(yb[:], y[:], biases_sb[:, 0:D], ALU.add).then_inc(yb_ready, 1)

            pool.memset(v_ring[:].rearrange("p n h d -> p (n h d)"), 1.0).then_inc(ones_set, 1)
            pool.wait_ge(ones_set, 1)
            pool.wait_ge(first_stats, 2 * TPC + 1)
            pool.tensor_tensor(first_scale[:], first_ve[:].rearrange("p t o -> p (t o)"), minus_half[:],
                               ALU.pow).then_inc(first_scale_ready, 1)

            def serve_quad(c, i, first=False):
                pre, post_ = PRE_SLOTS[c], POST_SLOTS[c]
                g_pre, g_post = TPC * (c + 1) + i, TPC * (c - 1) + i
                if c == 0:
                    pool.wait_ge(first_v_stored, TPC)
                else:
                    pool.wait_ge(v_stored, TPC * c)
                if pre:
                    rstd_x(g_pre)
                if post_:
                    gather_sums(g_post, c - 1, i)
                for kb in range(periods[c]):
                    n = first_period[c] + i * periods[c] + kb
                    if not (first and kb < V_RING):
                        pool.wait_ge(pv_done, n - V_RING + 1)
                    pool.tensor_copy(v_ring[:, kb % V_RING, :, 0:DK], v_all[:, kb, bass.ds(i * QUAD, QUAD), :]
                                     ).then_inc(v_ready, 1)
                    if "o" in post_.get(kb, ()):
                        rstd_y(g_post)
                    if "project" in pre.get(kb, ()):
                        low_parts(g_pre)

            serve_quad(0, 0, first=True)
            with pool.Fori(1, NQUAD) as i:
                serve_quad(0, i)
            for c in range(1, NCHUNK):
                if c == 1:
                    pool.wait_ge(result_out, 16)
                with pool.Fori(0, NQUAD) as i:
                    serve_quad(c, i)
            with pool.Fori(0, TPC) as i:
                gather_sums(TILES - TPC + i, NCHUNK - 1, i)
                rstd_y(TILES - TPC + i)


def kernel(**inputs):
    import concourse.bacc as bacc
    from concourse.bass_utils import run_bass_kernel_spmd

    from ml_dtypes import bfloat16 as bf16

    given = {name: np.asarray(a) for name, a in inputs.items()}

    def halves(w):
        return np.ascontiguousarray(w.reshape(KH, P, w.shape[1]).transpose(1, 0, 2))

    order = np.arange(D).reshape(H, KH, DK // KH).transpose(1, 2, 0).reshape(D)
    wq, wk, wv = (given[f"L0_attn_{n}_proj"] for n in "qkv")
    wo = given["L0_attn_o_proj"]
    row = np.arange(P)
    tail = np.zeros((TAIL, H, CHUNK), np.float32)
    k_tail, q_tail = tail.copy(), tail.copy()
    k_tail[0:SHIFT_ROWS] = 1.0
    q_tail[0] = -SHIFT
    arrays = {
        "x": np.ascontiguousarray(given["L0_attn_in_features"].reshape(TILES, P, D).transpose(1, 0, 2)),
        "wqkv": halves(np.concatenate([wq[order].T, wk[order].T, wv.T], 1)),
        "wo": halves(wo.T),
        "wffn": halves(np.concatenate([given["L0_ffn_W"].T, given["L0_ffn_lora_A"].reshape(E * R, D).T,
                                       given["L0_ffn_gate_w"].T], 1)),
        "lora_b": np.ascontiguousarray(given["L0_ffn_lora_B"].transpose(0, 2, 1).reshape(E * R, D)),
        "biases": np.ascontiguousarray(np.broadcast_to(
            np.concatenate([given["L0_ffn_b"], given["L0_ffn_gate_b"]])[None], (P, D + E))),
        "ident": np.eye(P, dtype=np.float32),
        "ident_bf": np.eye(P, dtype=np.float32).astype(bf16),
        "masks": np.stack([np.where(row[None, :] >= row[:, None], BIG, 0.0),
                           np.where(row[None, :] <= row[:, None], BIG, -BIG)], 1).astype(np.float32),
        "head_sum": (row[:, None] % H == np.arange(H)[None, :]).astype(np.float32).astype(bf16),
        "expert_ids": np.broadcast_to(np.arange(E, dtype=np.float32)[None], (P, E)).copy(),
        "k_tail": k_tail.astype(bf16),
        "q_tail": q_tail.astype(bf16),
    }
    nc = bacc.Bacc("TRN2", target_bir_lowering=False, num_devices=1)
    args = [nc.dram_tensor(n, a.shape, mybir.dt.from_np(a.dtype), kind="ExternalInput").ap()
            for n, a in arrays.items()]
    out = nc.dram_tensor("out", (TILES, P, D), F32, kind="ExternalOutput").ap()
    transformer_block(nc, *args, out)
    r = run_bass_kernel_spmd(nc, [arrays], core_ids=[0])
    return r.results[0]["out"].reshape(1, S, D)
```

```python
from contextlib import ExitStack

import numpy as np

import concourse.bass as bass
from concourse import mybir

F32 = mybir.dt.float32
BF16 = mybir.dt.bfloat16
I32 = mybir.dt.int32
U32 = mybir.dt.uint32
ALU = mybir.AluOpType
ACT = mybir.ActivationFunctionType
AX_X = mybir.AxisListType.X

P = 128
S, D = 2048, 256
H, DK = 16, 16
E, R = 8, 16
EPS = 1e-5
TILES = S // P
CHUNK = 512
NCHUNK = S // CHUNK
TPC = CHUNK // P
QUAD = 4
NQUAD = H // QUAD
KH = D // P
FFN = D + E * R + E

Q_SLOTS = (0, 0, 0, 1, 1, 1, 2)
K_SLOTS = (0, 1, 2, 0, 1, 2, 0)
K_RUNS = ((0, 2, 3), (6, 1, 1))
STACK = DK * len(Q_SLOTS)
SHIFT_ROWS = 3
TAIL = P - STACK

LAG = 2
RSTD_AT, GATHER_AT = 1, 0
WARM_UP = 13
PROBS = 4
V_RING = 4

BOUND, SHIFT = 40.0, 20.0
ROUNDING = 0.97
BIG = 3.0e38


class AfterAttention:

    def __init__(self, make, sums, bank, turn_bank, copied, first_tile):
        self.sums = sums
        self.bank, self.turn_bank = bank, turn_bank
        self.attn_t_ready, self.yT_ready, self.gatedT_ready = copied
        self.first_tile = first_tile
        self.inverse = make("inverse", [H], F32)
        self.attn_y = make("attn_y", [H, DK], F32)
        self.attn_t = make("attn_t", [KH, P], F32)
        self.y = make("y", [D], F32)
        self.yb = make("yb", [D], F32)
        self.bn2 = make("bn2", [6], F32)
        self.mv2 = make("mv2", [2], F32)
        self.ve2 = make("ve2", [1], F32)
        self.rstd2 = make("rstd2", [1], F32)
        self.yln = make("yln", [D], F32)
        self.yT = make("yT", [KH, P], F32)
        self.logits = make("logits", [E], F32)
        self.top = make("top", [8], F32)
        self.top_at = make("top_at", [8], U32)
        self.top_id = make("top_id", [2], F32)
        self.top_gap = make("top_gap", [1], F32)
        self.exp_gap = make("exp_gap", [1], F32)
        self.gate_den = make("gate_den", [1], F32)
        self.gate_of = make("gate_of", [2], F32)
        self.gates2 = make("gates2", [2, E], F32)
        self.gates = make("gates", [E], F32)
        self.gated = make("gated", [E, R], F32)
        self.gatedT = make("gatedT", [P], F32)
        self.result = make("result", [D], F32)


def transformer_block(nc, x, wqkv, wo, wffn, lora_b, biases, ident, ident_bf, masks, head_sum,
                      expert_ids, k_tail, q_tail, out):
    ctx = ExitStack()
    with ctx:
        def sb(name, shape, dt=F32):
            return ctx.enter_context(nc.sbuf_tensor(name, shape, dt))

        def bank(name, shape, dt=F32):
            return ctx.enter_context(nc.psum_tensor(name, shape, dt))

        def sem(name):
            return ctx.enter_context(nc.semaphore(name))

        parts_dram = nc.dram_tensor("parts_dram", (NCHUNK, 2, 3, KH, P, CHUNK), BF16, kind="Internal").ap()
        shift_dram = nc.dram_tensor("shift_dram", (NCHUNK, H, SHIFT_ROWS * TPC, P), BF16, kind="Internal").ap()

        x_sb = sb("x_sb", [P, TILES, D])
        wqkv_sb = sb("wqkv_sb", [P, KH, 3 * D])
        wo_sb = sb("wo_sb", [P, KH, D])
        wffn_sb = sb("wffn_sb", [P, KH, FFN])
        lora_b_sb = sb("lora_b_sb", [P, D])
        biases_sb = sb("biases_sb", [P, D + E])
        ident_sb = sb("ident_sb", [P, P])
        ident_bf_sb = sb("ident_bf_sb", [P, P], BF16)
        masks_sb = sb("masks_sb", [P, 2, P])
        head_sum_sb = sb("head_sum_sb", [P, H], BF16)
        expert_ids_sb = sb("expert_ids_sb", [P, E])
        hold_cell = sb("hold_cell", [1, 1])
        minus_half = sb("minus_half", [P, TPC])
        k_stack = sb("k_stack", [P, NCHUNK, H, CHUNK], BF16)
        q_stack = sb("q_stack", [P, 2, H, CHUNK], BF16)
        v_all = sb("v_all", [P, TILES, H, DK])
        attn = sb("attn", [P, NQUAD, TPC, P])

        v_ring = sb("v_ring", [P, V_RING, QUAD, 32])
        probs = sb("probs", [P, PROBS, QUAD, CHUNK])
        bn1 = sb("bn1", [P, 6])
        mv1 = sb("mv1", [P, 2])
        ve1 = sb("ve1", [P, 1])
        rstd1 = sb("rstd1", [P, 1])
        xln = sb("xln", [P, D])
        xT = sb("xT", [P, KH, P])
        parts = sb("parts", [P, 2, 3, KH, P], BF16)
        rest1 = sb("rest1", [P, 2, KH, P])
        clamped = sb("clamped", [P, 2, KH, P], BF16)
        norms = sb("norms", [H, 2, TILES])
        first_bn = sb("first_bn", [P, TPC, 6])
        first_mv = sb("first_mv", [P, TPC, 2])
        first_ve = sb("first_ve", [P, TPC, 1])
        first_scale = sb("first_scale", [P, TPC])
        first_rest = probs[:, 0]
        first_xln = probs[:, 1, 0:2].rearrange("p a (b d) -> p (a b) d", d=D)
        first_xT = probs[:, 1, 2:4]
        slots = 2 * 3 * KH
        first_parts = q_stack[:, 1, 0:slots].rearrange("p (k s m) t -> p k s m t", k=2, s=3)
        first_squares = q_stack[:, 1, slots:slots + 2 * KH]
        warm_up = probs[:, 2, 0, 0:CHUNK // 2].bitcast(BF16)
        norm_max = sb("norm_max", [H, 2])
        bound_sq = sb("bound_sq", [32, 32])
        bound_row = sb("bound_row", [32, 32])
        bound_max = sb("bound_max", [1, 1])
        is_bounded = sb("is_bounded", [1, NCHUNK], I32)
        row_max = sb("row_max", [P, 8])
        masked = sb("masked", [P, P])
        shift = sb("shift", [P, TPC])
        shift_rest = sb("shift_rest", [P, TPC])
        shift_parts = sb("shift_parts", [P, SHIFT_ROWS, TPC], BF16)
        shift_rows = sb("shift_rows", [SHIFT_ROWS * TPC, P], BF16)
        attn_in = sb("attn_in", [P, NQUAD, P])

        scores = [bank(f"scores{a}", [P, 2, CHUNK]) for a in range(2)]
        acc = bank("acc", [P, CHUNK])
        pre_a = bank("pre_a", [P, 2, D])
        pre_b = bank("pre_b", [P, 2, KH, P])
        post = bank("post", [P, CHUNK])

        first_banks = [acc[:], post[:], pre_a[:].rearrange("p a d -> p (a d)"),
                       pre_b[:].rearrange("p k m t -> p (k m t)")]

        weights_in = sem("weights_in")
        x_in = [sem(f"x_in{c}") for c in range(NCHUNK)]
        x_rest_in = sem("x_rest_in")
        ident_in = sem("ident_in")
        consts_in = sem("consts_in")
        post_weights_in = sem("post_weights_in")
        tails_in = [sem(f"tails_in{par}") for par in range(2)]
        const_set = sem("const_set")
        ones_set = sem("ones_set")
        warm_up_set = sem("warm_up_set")
        first_stats = sem("first_stats")
        first_scale_ready = sem("first_scale_ready")
        first_xln_ready = sem("first_xln_ready")
        first_xT_psum = sem("first_xT_psum")
        first_xT_ready = sem("first_xT_ready")
        first_qk_psum = sem("first_qk_psum")
        first_v_psum = sem("first_v_psum")
        first_high = sem("first_high")
        first_rest_ready = sem("first_rest_ready")
        first_middle = sem("first_middle")
        first_low = sem("first_low")
        first_clamped = sem("first_clamped")
        first_squared = sem("first_squared")
        first_norm_psum = sem("first_norm_psum")
        first_k_out = sem("first_k_out")
        stats1 = sem("stats1")
        rstd1_ready = sem("rstd1_ready")
        xln_ready = sem("xln_ready")
        xT_psum = sem("xT_psum")
        xT_ready = sem("xT_ready")
        qk_psum = sem("qk_psum")
        v_psum = sem("v_psum")
        v_stored = sem("v_stored")
        high_ready = sem("high_ready")
        split = sem("split")
        low_ready = sem("low_ready")
        norm_psum = sem("norm_psum")
        norms_clear = sem("norms_clear")
        norm_read = sem("norm_read")
        parts_out = sem("parts_out")
        q_in = sem("q_in")
        k_in = sem("k_in")
        bound_step = sem("bound_step")
        gen_scores = [sem(f"gen_scores{c}") for c in range(NCHUNK)]
        gen_max = [sem(f"gen_max{c}") for c in range(NCHUNK)]
        gen_read = [sem(f"gen_read{c}") for c in range(NCHUNK)]
        gen_turned = [sem(f"gen_turned{c}") for c in range(NCHUNK)]
        gen_rows = [sem(f"gen_rows{c}") for c in range(NCHUNK)]
        gen_out = [sem(f"gen_out{c}") for c in range(NCHUNK)]
        gen_in = [sem(f"gen_in{c}") for c in range(NCHUNK)]
        scores_ready = sem("scores_ready")
        exp_done = sem("exp_done")
        causal_done = sem("causal_done")
        v_ready = sem("v_ready")
        pv_done = sem("pv_done")
        acc_read = sem("acc_read")
        attn_in_ready = sem("attn_in_ready")
        turned_psum = sem("turned_psum")
        inverse_ready = sem("inverse_ready")
        attn_y_ready = sem("attn_y_ready")
        attn_t_psum = sem("attn_t_psum")
        attn_t_ready = sem("attn_t_ready")
        o_psum = sem("o_psum")
        stats2 = sem("stats2")
        rstd2_ready = sem("rstd2_ready")
        yb_ready = sem("yb_ready")
        yln_ready = sem("yln_ready")
        yT_psum = sem("yT_psum")
        yT_ready = sem("yT_ready")
        ffn_psum = sem("ffn_psum")
        route = sem("route")
        gate = sem("gate")
        gap_exp = sem("gap_exp")
        gatedT_psum = sem("gatedT_psum")
        gatedT_ready = sem("gatedT_ready")
        out_psum = sem("out_psum")
        tail_attn_t_ready = sem("tail_attn_t_ready")
        tail_yT_ready = sem("tail_yT_ready")
        tail_gatedT_ready = sem("tail_gatedT_ready")
        result_ready = sem("result_ready")
        result_out = sem("result_out")

        loop = AfterAttention(lambda name, shape, dt: sb(name, [P] + shape, dt)[:], attn_in, post[:], pre_a[:, 0, 0:P],
                              (attn_t_ready, yT_ready, gatedT_ready), 0)
        tail_banks = [post[:], scores[0][:, 0], scores[0][:, 1], scores[1][:, 0]]
        tail_turn_banks = [pre_a[:, 0, 0:P], pre_b[:, 0, 0, :], acc[:, 0:P], scores[1][:, 1, 0:P]]

        def carver(space):
            used = [0]

            def make(name, shape, dt):
                n = int(np.prod(shape))
                view = space[:, used[0]:used[0] + n]
                used[0] += n
                if len(shape) == 2:
                    view = view.rearrange("p (a b) -> p a b", b=shape[1])
                return view if dt == F32 else view.bitcast(dt)
            return make

        tail = [AfterAttention(carver(k_stack[:, t].rearrange("p h t -> p (h t)").bitcast(F32)), attn[:, t],
                               tail_banks[t], tail_turn_banks[t],
                               (tail_attn_t_ready, tail_yT_ready, tail_gatedT_ready), TILES - TPC)
                for t in range(TPC)]

        STATS1, SPLIT, BOUND_STEPS, STATS2, ROUTE, GATE = 3, 4, 5, 4, 5, 7
        Q_DMAS, K_DMAS = 3, 2

        periods = [TPC * (c + 1) for c in range(NCHUNK)]
        first_period = [NQUAD * sum(periods[:c]) for c in range(NCHUNK)]

        def span(c, kb):
            return max(0, kb - TPC * c) * P

        PRE_SLOTS = ({2: ["turn"], 3: ["project"], 4: ["norm"]},
                     {3: ["turn"], 4: ["project"], 5: ["norm"]},
                     {3: ["turn"], 4: ["project"], 6: ["norm"]},
                     {})
        POST_SLOTS = ({},
                      {2: ["turn_sums"], 3: ["turn_back", "o", "normalise"], 4: ["turn"], 6: ["ffn"], 7: ["gates"],
                       8: ["turn_gated"], 9: ["lora"]},
                      {2: ["turn_sums"], 3: ["turn_back"], 5: ["o", "normalise"], 7: ["turn"], 8: ["ffn"],
                       9: ["gates"], 11: ["turn_gated"], 12: ["lora"]},
                      {2: ["turn_sums"], 3: ["turn_back"], 5: ["o"], 7: ["normalise"], 9: ["turn"], 10: ["ffn"],
                       11: ["gates"], 14: ["turn_gated"], 16: ["lora"]})
        DECIDE_AT = (3, 4, 3, None)

        def next_tile(c, i):
            return TPC * (c + 1) + 1 + i

        def pre_slots(c, i):
            return {} if c == NCHUNK - 2 and isinstance(i, int) and i == NQUAD - 1 else PRE_SLOTS[c]

        def for_quads(engine, c, body, peel_last=False):
            count = NQUAD - 1 if peel_last or c == NCHUNK - 2 else NQUAD
            with engine.Fori(0, count) as i:
                body(c, i)
            if count < NQUAD:
                body(c, NQUAD - 1)

        TAIL_STAGES = {"turn_sums": -2, "turn_back": 0.5, "o": 1.5, "normalise": 3, "turn": 4,
                       "ffn": 5, "gates": 6.5, "turn_gated": 8.5, "lora": 9.5}
        TAIL_STEP = 1
        TAIL_ORDER = sorted(((name, t) for name in TAIL_STAGES for t in range(TPC)),
                            key=lambda stage: TAIL_STAGES[stage[0]] + TAIL_STEP * stage[1])

        def sums_of_quad(c, i):
            return attn[:, bass.ds(i, 1), :, :] if c % 2 == 0 else attn[:, :, bass.ds(i, 1), :]

        def sums_of_tile(c, i):
            return attn[:, :, bass.ds(i, 1), :] if c % 2 == 0 else attn[:, bass.ds(i, 1), :, :]

        block = ctx.enter_context(nc.Block())

        @block.sync
        def _(sp):
            sp.dma_start(x_sb[:, 0:2, :], x[:, 0:2, :]).then_inc(x_in[0], 16)
            sp.dma_start(x_sb[:, 2:TPC, :], x[:, 2:TPC, :]).then_inc(x_rest_in, 16)
            sp.dma_start(ident_sb[:], ident).then_inc(ident_in, 16)
            sp.dma_start(wqkv_sb[:], wqkv).then_inc(weights_in, 16)
            sp.dma_start(x_sb[:, TPC:2 * TPC, :], x[:, TPC:2 * TPC, :]).then_inc(x_in[1], 16)
            sp.dma_start(head_sum_sb[:], head_sum).then_inc(consts_in, 16)
            sp.dma_start(masks_sb[:], masks).then_inc(consts_in, 16)
            sp.dma_start(ident_bf_sb[:], ident_bf).then_inc(consts_in, 16)
            sp.dma_start(q_stack[STACK:P, 0], q_tail).then_inc(tails_in[0], 16)
            for c in range(NCHUNK):
                sp.dma_start(k_stack[STACK:P, c], k_tail).then_inc(tails_in[0], 16)
            def load_rest():
                for c in range(2, NCHUNK):
                    sp.dma_start(x_sb[:, c * TPC:(c + 1) * TPC, :], x[:, c * TPC:(c + 1) * TPC, :]
                                 ).then_inc(x_in[c], 16)
                sp.dma_start(wo_sb[:], wo).then_inc(post_weights_in, 16)
                sp.dma_start(wffn_sb[:], wffn).then_inc(post_weights_in, 16)
                sp.dma_start(lora_b_sb[:], lora_b).then_inc(post_weights_in, 16)
                sp.dma_start(biases_sb[:], biases).then_inc(result_out, 16)
                sp.dma_start(expert_ids_sb[:], expert_ids).then_inc(post_weights_in, 16)

            def store_parts(c, i):
                u = (c - 1) * TPC + i
                first_token = i * P if isinstance(i, int) else sp.snap(i * P)
                sp.wait_ge(low_ready, u + 1)
                sp.dma_start(parts_dram[c, :, :, :, :, bass.ds(first_token, P)].rearrange("k s m p t -> p (k s m) t"),
                             parts[:].rearrange("p k s m t -> p (k s m) t")).then_inc(parts_out, 16)

            def part_rows(c, k, heads):
                return parts_dram[c, k].rearrange("s m (d h) t -> (s m d) h t", h=H)[:, heads, :]

            def load_stacks(c, quad):
                first = c == 0 and isinstance(quad, int)
                heads = bass.ds(quad * QUAD if isinstance(quad, int) else sp.snap(quad * QUAD), QUAD)
                if first:
                    sp.wait_ge(parts_out, 16)
                else:
                    sp.wait_ge(q_in, 16 * Q_DMAS * (NQUAD * c + quad))
                rows = part_rows(c, 0, heads)
                for part in range(3):
                    first_slot, n = Q_SLOTS.index(part), Q_SLOTS.count(part)
                    sp.dma_start(q_stack[first_slot * DK:(first_slot + n) * DK, c % 2, heads, :],
                                 rows[part * DK:(part + 1) * DK].unsqueeze(0).to_broadcast([n, DK, QUAD, CHUNK])
                                 ).then_inc(q_in, 16)
                if first:
                    sp.wait_ge(first_k_out, 16)
                else:
                    sp.wait_ge(k_in, 16 * K_DMAS * (NQUAD * c + quad))
                rows = part_rows(c, 1, heads)
                for first_slot, n, k in K_RUNS:
                    sp.dma_start(k_stack[first_slot * DK:(first_slot + n * k) * DK, c, heads, :],
                                 rows[0:k * DK].unsqueeze(0).to_broadcast([n, k * DK, QUAD, CHUNK])
                                 ).then_inc(k_in, 16)

            def store_shifts(c):
                sp.wait_ge(q_in, 16 * Q_DMAS * NQUAD * (c + 1))
                sp.wait_ge(tails_in[c % 2], 16 * (1 if c % 2 else 1 + NCHUNK))
                with sp.Fori(0, H) as h:
                    sp.wait_ge(gen_rows[c], h + 1)
                    sp.dma_start(shift_dram[c, h], shift_rows[:]).then_inc(gen_out[c], 16)
                    sp.wait_ge(gen_out[c], 16 * (h + 1))
                    sp.dma_start(q_stack[STACK:STACK + SHIFT_ROWS, c % 2, h, :],
                                 shift_dram[c, h].rearrange("(s i) t -> s (i t)", s=SHIFT_ROWS)
                                 ).then_inc(gen_in[c], 16)

            for k in range(2):
                sp.wait_ge(first_low, KH * (k + 1))
                sp.dma_start(parts_dram[0, k].rearrange("s m p t -> p (s m) t"),
                             first_parts[:, k].rearrange("p s m t -> p (s m) t")
                             ).then_inc(first_k_out if k else parts_out, 16)

            def store_result(g):
                row = g if isinstance(g, int) else sp.snap(g)
                sp.wait_ge(result_ready, g + 2)
                w = tail[g - (TILES - TPC)] if isinstance(g, int) and g >= TILES - TPC else loop
                sp.dma_start(out[row], w.result).then_inc(result_out, 16)

            def finish_chunk(c):
                if c + 1 < NCHUNK:
                    sp.wait_ge(parts_out, 16 * (1 + TPC * (c + 1)))
                    load_stacks(c + 1, 0)
                if c + 2 < NCHUNK:
                    store_parts(c + 2, 0)

            def store_last_result(c):
                if c > 0:
                    store_result(TPC * c - 1)

            load_stacks(0, 0)
            for c in range(NCHUNK):
                sp.wait_ge(bound_step, BOUND_STEPS * (1 + NQUAD * c))
                if c == 0:
                    sp.dma_start(q_stack[STACK:P, 1], q_tail).then_inc(tails_in[1], 16)
                    load_rest()
                    store_parts(1, 0)
                bounded = sp.value_load(is_bounded[0:1, c:c + 1], min_val=0, max_val=1)
                with sp.If(bounded == 0):
                    with sp.Fori(1, NQUAD) as quad:
                        load_stacks(c, quad)
                    store_shifts(c)
                    store_last_result(c - 1)
                    with sp.Fori(1, TPC) as i:
                        if c + 1 < NCHUNK:
                            store_parts(c + 1, i)
                        if c > 0:
                            store_result(TPC * (c - 1) + i - 1)
                    finish_chunk(c)
                with sp.If(bounded == 1):
                    store_last_result(c - 1)
                    with sp.Fori(1, NQUAD) as quad:
                        load_stacks(c, quad)
                        if c + 1 < NCHUNK:
                            store_parts(c + 1, quad)
                        if c > 0:
                            store_result(TPC * (c - 1) + quad - 1)
                    finish_chunk(c)
            store_last_result(NCHUNK - 1)
            for t in range(TPC):
                store_result(TILES - TPC + t)
            sp.wait_ge(parts_out, 16 * (1 + TILES - TPC))
            sp.wait_ge(result_out, 16 * (TILES + 1))

        @block.tensor
        def _(pe):
            def project_first_chunk():
                pe.wait_ge(warm_up_set, 1)
                for _ in range(WARM_UP):
                    pe.matmul(acc[:], warm_up[:, 0:P], warm_up, start=True, stop=True)
                pe.wait_ge(ident_in, 16)
                for t in range(TPC):
                    pe.wait_ge(first_xln_ready, t + 1)
                    for k in range(KH):
                        m = pe.transpose(scores[t // 2][:, t % 2, k * P:(k + 1) * P],
                                         first_xln[:, t, k * P:(k + 1) * P], ident_sb[:])
                    m.then_inc(first_xT_psum, 1)
                pe.wait_ge(weights_in, 16)
                pe.wait_ge(const_set, 1)
                pe.wait_ge(first_xT_ready, TPC)
                for n in range(2 * KH):
                    for k in range(KH):
                        m = pe.matmul(first_banks[n], wqkv_sb[:, k, n * P:(n + 1) * P], first_xT[:, k, :],
                                      start=(k == 0), stop=(k == KH - 1))
                    m.then_inc(first_qk_psum, 1)
                for t in range(TPC):
                    for k in range(KH):
                        m = pe.matmul(scores[t // 2][:, t % 2, 0:D], first_xT[:, k, t * P:(t + 1) * P],
                                      wqkv_sb[:, k, 2 * D:3 * D], start=(k == 0), stop=(k == KH - 1))
                    m.then_inc(first_v_psum, 1)
                turn_x(TPC)
                pe.wait_ge(consts_in, 16 * 3)
                pe.wait_ge(first_squared, 2 * KH)
                for a in range(2):
                    for k in range(KH):
                        m = pe.matmul(first_banks[a][0:H], head_sum_sb[:], first_squares[:, a * KH + k, :],
                                      start=(k == 0), stop=(k == KH - 1))
                    m.then_inc(first_norm_psum, 1)
                pe.wait_ge(v_stored, TPC)
                project(TPC)

            def turn_x(g):
                pe.wait_ge(xln_ready, g - TPC + 1)
                if isinstance(g, int):
                    pe.wait_ge(first_rest_ready, 2 * KH)
                for k in range(KH):
                    t = pe.transpose(pre_a[:, 0, k * P:(k + 1) * P], xln[:, k * P:(k + 1) * P], ident_sb[:])
                t.then_inc(xT_psum, 1)

            def project(g):
                pe.wait_ge(xT_ready, g - TPC + 1)
                for n in range(2 * KH):
                    for k in range(KH):
                        m = pe.matmul(pre_b[:, n // KH, n % KH, :], wqkv_sb[:, k, n * P:(n + 1) * P], xT[:, k, :],
                                      start=(k == 0), stop=(k == KH - 1))
                m.then_inc(qk_psum, 1)
                for k in range(KH):
                    m = pe.matmul(pre_a[:, 1, :], xT[:, k, :], wqkv_sb[:, k, 2 * D:3 * D],
                                  start=(k == 0), stop=(k == KH - 1))
                m.then_inc(v_psum, 1)

            def sum_squares(g):
                pe.wait_ge(split, SPLIT * (g - TPC + 1))
                for k in range(KH):
                    m = pe.matmul(pre_b[0:H, :, 0, :], head_sum_sb[:], clamped[:, :, k, :],
                                  start=(k == 0), stop=(k == KH - 1))
                m.then_inc(norm_psum, 1)

            PRE = {"turn": turn_x, "project": project, "norm": sum_squares}

            def turn_sums(g, w):
                if w is loop:
                    pe.wait_ge(attn_in_ready, g + 1)
                    pe.wait_ge(result_ready, g + 1)
                else:
                    pe.wait_ge(acc_read, NQUAD * NCHUNK + 1)
                    pe.wait_ge(result_ready, TILES - TPC + 1)
                for q in range(NQUAD):
                    t = pe.transpose(w.bank[:, q * P:(q + 1) * P], w.sums[:, q, :], ident_sb[:])
                t.then_inc(turned_psum, 1)

            def turn_back(g, w):
                pe.wait_ge(attn_y_ready, g + 1)
                for k in range(KH):
                    t = pe.transpose(w.bank[:, k * P:(k + 1) * P],
                                     w.attn_y.rearrange("p h d -> p (h d)")[:, k * P:(k + 1) * P], ident_sb[:])
                t.then_inc(attn_t_psum, 1)

            def o_proj(g, w):
                pe.wait_ge(w.attn_t_ready, g - w.first_tile + 1)
                for k in range(KH):
                    m = pe.matmul(w.bank[:, 0:D], w.attn_t[:, k, :], wo_sb[:, k, :], start=(k == 0), stop=(k == KH - 1))
                m.then_inc(o_psum, 1)

            def turn_y(g, w):
                pe.wait_ge(yln_ready, g + 1)
                for k in range(KH):
                    t = pe.transpose(w.bank[:, D + k * P:D + (k + 1) * P], w.yln[:, k * P:(k + 1) * P], ident_sb[:])
                t.then_inc(yT_psum, 1)

            def ffn(g, w):
                pe.wait_ge(w.yT_ready, g - w.first_tile + 1)
                for k in range(KH):
                    m = pe.matmul(w.bank[:, 0:FFN], w.yT[:, k, :], wffn_sb[:, k, :], start=(k == 0), stop=(k == KH - 1),
                                  skip_group_check=True)
                m.then_inc(ffn_psum, 1)

            def turn_gated(g, w):
                pe.wait_ge(gate, GATE * (g + 1))
                pe.transpose(w.turn_bank, w.gated.rearrange("p e r -> p (e r)"), ident_sb[:]
                             ).then_inc(gatedT_psum, 1)

            def lora(g, w):
                pe.wait_ge(w.gatedT_ready, g - w.first_tile + 1)
                pe.matmul(w.bank[:, 0:D], w.gatedT, lora_b_sb[:], start=False, stop=True,
                          skip_group_check=True).then_inc(out_psum, 1)

            POST = {"turn_sums": turn_sums, "turn_back": turn_back, "o": o_proj, "turn": turn_y, "ffn": ffn,
                    "turn_gated": turn_gated, "lora": lora}

            def row_maxima(c):
                with pe.Fori(0, H) as h:
                    for i in range(TPC):
                        if i > 0:
                            pe.wait_ge(gen_read[c], TPC * h + i)
                        lhs = q_stack[0:STACK, c % 2, h, i * P:(i + 1) * P]
                        for kc in range(c + 1):
                            n = CHUNK if kc < c else (i + 1) * P
                            m = pe.matmul(scores[kc // 2][:, kc % 2, 0:n], lhs,
                                          k_stack[0:STACK, kc, h, 0:n], start=True, stop=True)
                        m.then_inc(gen_scores[c], 1)
                    pe.wait_ge(gen_max[c], h + 1)
                    pe.transpose(pre_b[0:SHIFT_ROWS * TPC, 0, 0, 0:P // 2].bitcast(BF16),
                                 shift_parts[:].rearrange("p s i -> p (s i)"), ident_bf_sb[:]
                                 ).then_inc(gen_turned[c], 1)
                pe.wait_ge(gen_in[c], 16 * H)

            def qk(c, i, kb, a):
                quad_no = NQUAD * c + i
                n, lo = first_period[c] + i * periods[c] + kb, span(c, kb)
                if a == 0 and kb == 0:
                    pe.wait_ge(q_in, 16 * Q_DMAS * (quad_no + 1))
                if a == 0 and kb == TPC * c:
                    pe.wait_ge(k_in, 16 * K_DMAS * (quad_no + 1))
                if not (isinstance(n, int) and n == 0):
                    pe.wait_ge(exp_done, 2 * n + a - 1)
                for j in range(2):
                    head = i * QUAD + 2 * a + j
                    m = pe.matmul(scores[a][:, j, lo:CHUNK],
                                  k_stack[:, kb // TPC, head, kb % TPC * P:(kb % TPC + 1) * P],
                                  q_stack[:, c % 2, head, lo:CHUNK], start=True, stop=True)
                m.then_inc(scores_ready, 1)

            def pv(c, i, kb, first, end):
                quad_no = NQUAD * c + i
                n = first_period[c] + i * periods[c] + kb
                lo = max(span(c, kb), first)
                if first == 0:
                    pe.wait_ge(exp_done, 2 * n + 2)
                    pe.wait_ge(v_ready, n + 1)
                    if kb >= TPC * c:
                        pe.wait_ge(causal_done, TPC * quad_no + kb - TPC * c + 1)
                    if kb == 0:
                        pe.wait_ge(acc_read, quad_no + 1)
                for j in range(QUAD):
                    m = pe.matmul(acc[32 * j:32 * j + 32, lo:end], v_ring[:, kb % V_RING, j, :],
                                  probs[:, kb % PROBS, j, lo:end], start=(kb == 0), stop=(kb == periods[c] - 1),
                                  tile_position=(0, 32 * j), skip_group_check=True)
                if end == CHUNK:
                    m.then_inc(pv_done, 1)

            def open_chunk(c):
                if c < 2:
                    pe.wait_ge(tails_in[c], 16 * (1 if c else 1 + NCHUNK))
                if c == 1:
                    pe.wait_ge(post_weights_in, 16 * 4)
                pe.wait_ge(bound_step, BOUND_STEPS * (1 + NQUAD * c))
                bounded = pe.value_load(is_bounded[0:1, c:c + 1], min_val=0, max_val=1)
                with pe.If(bounded == 0):
                    pe.wait_ge(q_in, 16 * Q_DMAS * NQUAD * (c + 1))
                    pe.wait_ge(k_in, 16 * K_DMAS * NQUAD * (c + 1))
                    if c > 0:
                        pe.wait_ge(exp_done, 2 * first_period[c])
                    row_maxima(c)

            def attend(c, i):
                last = isinstance(i, int)
                for k in range(LAG, periods[c] + LAG):
                    if k < periods[c]:
                        ahead = (c, i, k)
                    elif not last:
                        ahead = (c, i + 1, k - periods[c])
                    elif c + 1 < NCHUNK:
                        ahead = (c + 1, 0, k - periods[c])
                        if k == periods[c]:
                            open_chunk(c + 1)
                    else:
                        ahead = None
                    if ahead:
                        qk(*ahead, 0)
                    kb = k - LAG
                    is_cut = 0 < kb and span(c, kb) < CHUNK // 2
                    pv(c, i, kb, 0, CHUNK // 2 if is_cut else CHUNK)
                    if ahead:
                        qk(*ahead, 1)
                    for name in pre_slots(c, i).get(k, ()):
                        PRE[name](next_tile(c, i))
                    for name in POST_SLOTS[c].get(k, ()):
                        if name in POST:
                            POST[name](TPC * (c - 1) + i, loop)
                    if is_cut:
                        pv(c, i, kb, CHUNK // 2, CHUNK)

            project_first_chunk()
            open_chunk(0)
            for kb in range(LAG):
                for a in range(2):
                    qk(0, 0, kb, a)
                if kb == 0:
                    sum_squares(TPC)
            for c in range(NCHUNK):
                with pe.Fori(0, NQUAD - 1) as i:
                    attend(c, i)
                attend(c, NQUAD - 1)
            for name, t in TAIL_ORDER:
                if name in POST:
                    POST[name](TILES - TPC + t, tail[t])

        @block.scalar
        def _(act):
            def exp_gap_of(g, w):
                act.wait_ge(route, ROUTE * g + 4)
                act.activation(w.exp_gap, w.top_gap, ACT.Exp).then_inc(gap_exp, 1)

            def store_attn_t(g, w):
                act.wait_ge(attn_t_psum, g + 1)
                act.copy(w.attn_t.rearrange("p k t -> p (k t)"), w.bank[:, 0:D]).then_inc(tail_attn_t_ready, 1)

            def store_yT(g, w):
                act.wait_ge(yT_psum, g + 1)
                act.copy(w.yT.rearrange("p k t -> p (k t)"), w.bank[:, D:2 * D]).then_inc(tail_yT_ready, 1)

            def store_gatedT(g, w):
                act.wait_ge(gatedT_psum, g + 1)
                act.copy(w.gatedT, w.turn_bank).then_inc(tail_gatedT_ready, 1)

            for t in range(TPC):
                act.wait_ge(first_xT_psum, t + 1)
                act.copy(first_xT[:, :, t * P:(t + 1) * P],
                         scores[t // 2][:, t % 2, 0:D].rearrange("p (k t) -> p k t", k=KH)
                         ).then_inc(first_xT_ready, 1)
            for n in range(2 * KH + 1):
                if n < 2 * KH:
                    act.wait_ge(first_qk_psum, n + 1)
                    act.copy(first_parts[:, n // KH, 0, n % KH, :], first_banks[n]).then_inc(first_high, 1)
                if n > 0:
                    act.wait_ge(first_rest_ready, n)
                    act.copy(first_parts[:, (n - 1) // KH, 1, (n - 1) % KH, :], first_rest[:, n - 1]
                             ).then_inc(first_middle, 1)
            for t in range(TPC):
                act.wait_ge(first_v_psum, t + 1)
                act.copy(v_all[:, t].rearrange("p h d -> p (h d)"), scores[t // 2][:, t % 2, 0:D]
                         ).then_inc(v_stored, 1)

            def store_projected(g):
                act.wait_ge(qk_psum, g - TPC + 1)
                act.wait_ge(parts_out, 16 * (g - TPC + 1))
                act.copy(parts[:, :, 0], pre_b[:]).then_inc(high_ready, 1)
                act.wait_ge(v_psum, g - TPC + 1)
                act.copy(v_all[:, bass.ds(g, 1)].rearrange("p o h d -> p o (h d)"), pre_a[:, 1:2, :]
                         ).then_inc(v_stored, 1)

            store_projected(TPC)

            def exponentials(c, i):
                for kb in range(periods[c]):
                    n, lo = first_period[c] + i * periods[c] + kb, span(c, kb)
                    for a in range(2):
                        act.wait_ge(scores_ready, 2 * n + a + 1)
                        act.activation(probs[:, kb % PROBS, 2 * a:2 * a + 2, lo:CHUNK], scores[a][:, :, lo:CHUNK],
                                       ACT.Exp).then_inc(exp_done, 1)
                    if "project" in pre_slots(c, i).get(kb, ()):
                        store_projected(next_tile(c, i))
                    if "ffn" in POST_SLOTS[c].get(kb, ()):
                        exp_gap_of(TPC * (c - 1) + i, loop)

            for c in range(NCHUNK):
                for_quads(act, c, exponentials)
            TAIL = {"turn_back": store_attn_t, "turn": store_yT, "ffn": exp_gap_of, "turn_gated": store_gatedT}
            for name, t in TAIL_ORDER:
                if name in TAIL:
                    TAIL[name](TILES - TPC + t, tail[t])

        @block.vector
        def _(dve):
            dve.memset(warm_up, 0.0).then_inc(warm_up_set, 1)
            dve.memset(minus_half[:], -0.5).then_inc(acc_read, 1)
            dve.memset(bound_sq[:], 0.0).then_inc(result_ready, 1)
            dve.memset(norms[:], 0.0).then_inc(norms_clear, 1)
            def hold_here():
                dve.memset(hold_cell[:], 0.0)

            def project_first_chunk():
                for t in range(TPC):
                    if t % 2 == 0:
                        dve.wait_ge(x_rest_in if t else x_in[0], 16)
                    dve.bn_stats(first_bn[:, t, :], x_sb[:, t, :]).then_inc(first_stats, 1)
                for t in range(TPC):
                    dve.wait_ge(first_stats, TPC)
                    dve.bn_aggr(first_mv[:, t, :], first_bn[:, t, :]).then_inc(first_stats, 1)
                dve.wait_ge(first_stats, 2 * TPC)
                dve.tensor_scalar(first_ve[:], first_mv[:, :, 1:2], EPS, None, ALU.add).then_inc(first_stats, 1)
                dve.wait_ge(first_scale_ready, 1)
                for t in range(TPC):
                    dve.tensor_scalar(first_xln[:, t, :], x_sb[:, t, :], first_mv[:, t, 0:1], first_scale[:, t:t + 1],
                                      ALU.subtract, ALU.mult).then_inc(first_xln_ready, 1)
                dve.wait_ge(weights_in, 16)
                dve.tensor_scalar(wqkv_sb[:, :, 0:D], wqkv_sb[:, :, 0:D], float(DK) ** -0.5, None,
                                  ALU.mult).then_inc(const_set, 1)
                dve.wait_ge(x_in[1], 16)
                measure_x(TPC)
                normalise_x(TPC)
                for n in range(2 * KH + 1):
                    if n < 2 * KH:
                        dve.wait_ge(first_high, n + 1)
                        dve.tensor_tensor(first_rest[:, n], first_banks[n], first_parts[:, n // KH, 0, n % KH, :],
                                          ALU.subtract).then_inc(first_rest_ready, 1)
                    if n > 0:
                        dve.wait_ge(first_middle, n)
                        dve.tensor_tensor(first_parts[:, (n - 1) // KH, 2, (n - 1) % KH, :], first_rest[:, n - 1],
                                          first_parts[:, (n - 1) // KH, 1, (n - 1) % KH, :],
                                          ALU.subtract).then_inc(first_low, 1)
                for n in range(2 * KH):
                    dve.tensor_scalar(first_squares[:, n], first_parts[:, n // KH, 0, n % KH, :], 1e15, -1e15,
                                      ALU.min, ALU.max).then_inc(first_clamped, 1)
                for n in range(2 * KH):
                    dve.wait_ge(first_clamped, n + 1)
                    dve.tensor_tensor(first_squares[:, n], first_squares[:, n], first_squares[:, n],
                                      ALU.mult).then_inc(first_squared, 1)
                store_xT(TPC)
                dve.wait_ge(norms_clear, 1)
                for a in range(2):
                    dve.wait_ge(first_norm_psum, a + 1)
                    dve.tensor_reduce(norms[:, a, 0:TPC], first_banks[a][0:H].rearrange("h (i t) -> h i t", i=TPC),
                                      AX_X, ALU.max).then_inc(norm_read, 1)

            def measure_x(g):
                dve.bn_stats(bn1[:], x_sb[:, g, :]).then_inc(stats1, 1)
                dve.wait_ge(stats1, STATS1 * (g - TPC) + 1)
                hold_here()
                dve.bn_aggr(mv1[:], bn1[:]).then_inc(stats1, 1)
                dve.wait_ge(stats1, STATS1 * (g - TPC) + 2)
                dve.tensor_scalar(ve1[:], mv1[:, 1:2], EPS, None, ALU.add).then_inc(stats1, 1)

            def normalise_x(g):
                dve.wait_ge(rstd1_ready, g - TPC + 1)
                dve.tensor_scalar(xln[:], x_sb[:, g, :], mv1[:, 0:1], rstd1[:], ALU.subtract,
                                  ALU.mult).then_inc(xln_ready, 1)

            def store_xT(g):
                dve.wait_ge(xT_psum, g - TPC + 1)
                dve.tensor_copy(xT[:].rearrange("p k t -> p (k t)"), pre_a[:, 0, :]).then_inc(xT_ready, 1)

            def split_qk(g):
                base = SPLIT * (g - TPC)
                dve.wait_ge(high_ready, g - TPC + 1)
                high, middle = parts[:, :, 0], parts[:, :, 1]
                dve.tensor_tensor(rest1[:], pre_b[:], high, ALU.subtract).then_inc(split, 1)
                dve.tensor_scalar(clamped[:], high, 1e15, -1e15, ALU.min, ALU.max).then_inc(split, 1)
                dve.wait_ge(split, base + 2)
                dve.tensor_copy(middle, rest1[:]).then_inc(split, 1)
                dve.tensor_tensor(clamped[:], clamped[:], clamped[:], ALU.mult).then_inc(split, 1)

            def read_norms(g):
                dve.wait_ge(norm_psum, g - TPC + 1)
                dve.tensor_reduce(norms[:, :, bass.ds(g, 1)], pre_b[0:H, :, 0, :], AX_X, ALU.max).then_inc(norm_read, 1)

            def decide_bound(c, n):
                base = BOUND_STEPS * n
                dve.wait_ge(norm_read, 2 + n)
                dve.tensor_reduce(norm_max[:], norms[:, :, 0:TPC * (c + 1)], AX_X, ALU.max).then_inc(bound_step, 1)
                dve.wait_ge(bound_step, base + 1)
                dve.tensor_scalar(bound_sq[0:H, 0:1], norm_max[:, 0:1], norm_max[:, 1:2], None,
                                  ALU.mult).then_inc(bound_step, 1)
                dve.wait_ge(bound_step, base + 2)
                hold_here()
                dve.transpose(bound_row[:], bound_sq[:]).then_inc(bound_step, 1)
                dve.wait_ge(bound_step, base + 3)
                dve.tensor_reduce(bound_max[:], bound_row[0:1, 0:H], AX_X, ALU.max).then_inc(bound_step, 1)
                dve.wait_ge(bound_step, base + 4)
                dve.tensor_scalar(is_bounded[:, c:c + 1], bound_max[:], BOUND * BOUND * ROUNDING, None,
                                  ALU.is_le).then_inc(bound_step, 1)

            def shifts(c):
                step = 0
                with dve.Fori(0, H) as h:
                    for i in range(TPC):
                        done = h * (TPC * GEN_STEPS + GEN_SPLIT) + i * GEN_STEPS
                        step = gen_step[c]
                        dve.memset(row_max[:], -BIG).then_inc(step, 1)
                        dve.wait_ge(gen_scores[c], TPC * h + i + 1)
                        dve.wait_ge(step, done + 1)
                        dve.tensor_tensor(masked[:], scores[c // 2][:, c % 2, i * P:(i + 1) * P], masks_sb[:, 1, :],
                                          ALU.min).then_inc(step, 1)
                        for kc in range(c):
                            dve.tensor_reduce(row_max[:, kc:kc + 1], scores[kc // 2][:, kc % 2, :], AX_X, ALU.max)
                        if i > 0:
                            dve.tensor_reduce(row_max[:, 4:5], scores[c // 2][:, c % 2, 0:i * P], AX_X, ALU.max)
                        dve.wait_ge(step, done + 2)
                        dve.tensor_reduce(row_max[:, 5:6], masked[:], AX_X, ALU.max).then_inc(gen_read[c], 1)
                        dve.wait_ge(gen_read[c], TPC * h + i + 1)
                        dve.tensor_reduce(masked[:, 0:1], row_max[:], AX_X, ALU.max).then_inc(step, 1)
                        dve.wait_ge(step, done + 3)
                        dve.tensor_scalar(shift[:, i:i + 1], masked[:, 0:1], -1.0, None, ALU.mult).then_inc(step, 1)
                    done = h * (TPC * GEN_STEPS + GEN_SPLIT) + TPC * GEN_STEPS
                    dve.wait_ge(step, done)
                    dve.tensor_copy(shift_parts[:, 0], shift[:]).then_inc(step, 1)
                    dve.wait_ge(step, done + 1)
                    dve.tensor_tensor(shift_rest[:], shift[:], shift_parts[:, 0], ALU.subtract).then_inc(step, 1)
                    dve.wait_ge(step, done + 2)
                    dve.tensor_copy(shift_parts[:, 1], shift_rest[:]).then_inc(step, 1)
                    dve.wait_ge(step, done + 3)
                    dve.tensor_tensor(shift_parts[:, 2], shift_rest[:], shift_parts[:, 1],
                                      ALU.subtract).then_inc(gen_max[c], 1)
                    dve.wait_ge(gen_turned[c], h + 1)
                    dve.tensor_copy(shift_rows[:], pre_b[0:SHIFT_ROWS * TPC, 0, 0, 0:P // 2].bitcast(BF16)
                                    ).then_inc(gen_rows[c], 1)
                    dve.wait_ge(gen_out[c], 16 * (h + 1))

            def clear_later_keys(c, i, kb):
                n, j = first_period[c] + i * periods[c] + kb, kb - TPC * c
                dve.wait_ge(exp_done, 2 * n + 2)
                tile = probs[:, kb % PROBS, :, j * P:(j + 1) * P]
                mask = masks_sb[:, 0:1, :].to_broadcast([P, QUAD, P])
                dve.tensor_tensor(tile, tile, mask, ALU.min).then_inc(causal_done, 1)

            def keep_sums(c, i):
                dve.wait_ge(pv_done, first_period[c] + (i + 1) * periods[c])
                dve.tensor_copy(sums_of_quad(c, i), acc[:].rearrange("p (a t) -> p a t", a=TPC).unsqueeze(
                    1 if c % 2 == 0 else 2)).then_inc(acc_read, 1)

            def divide(g, w):
                turned = w.bank.rearrange("p (h d) -> p h d", d=32)
                dve.wait_ge(turned_psum, g + 1)
                dve.reciprocal(w.inverse.unsqueeze(2), turned[:, :, DK:DK + 1]).then_inc(inverse_ready, 1)
                dve.wait_ge(inverse_ready, g + 1)
                dve.tensor_tensor(w.attn_y, turned[:, :, 0:DK], w.inverse.unsqueeze(2).to_broadcast([P, H, DK]),
                                  ALU.mult).then_inc(attn_y_ready, 1)

            def store_attn_t(g, w):
                dve.wait_ge(attn_t_psum, g + 1)
                dve.tensor_copy(w.attn_t.rearrange("p k t -> p (k t)"), w.bank[:, 0:D]).then_inc(attn_t_ready, 1)

            def residual_and_stats(g, w):
                base = STATS2 * g
                dve.wait_ge(o_psum, g + 1)
                dve.tensor_tensor(w.y, w.bank[:, 0:D], x_sb[:, g, :], ALU.add).then_inc(stats2, 1)
                dve.wait_ge(stats2, base + 1)
                dve.bn_stats(w.bn2, w.y).then_inc(stats2, 1)
                dve.wait_ge(stats2, base + 2)
                hold_here()
                dve.bn_aggr(w.mv2, w.bn2).then_inc(stats2, 1)
                dve.wait_ge(stats2, base + 3)
                dve.tensor_scalar(w.ve2, w.mv2[:, 1:2], EPS, None, ALU.add).then_inc(stats2, 1)

            def normalise_y(g, w):
                dve.wait_ge(rstd2_ready, g + 1)
                dve.tensor_scalar(w.yln, w.y, w.mv2[:, 0:1], w.rstd2, ALU.subtract, ALU.mult).then_inc(yln_ready, 1)

            def store_yT(g, w):
                dve.wait_ge(yT_psum, g + 1)
                dve.tensor_copy(w.yT.rearrange("p k t -> p (k t)"), w.bank[:, D:2 * D]).then_inc(yT_ready, 1)

            def route_tokens(g, w):
                base = ROUTE * g
                dve.wait_ge(result_out, 16)
                dve.wait_ge(ffn_psum, g + 1)
                dve.tensor_tensor(w.logits, w.bank[:, D + E * R:FFN], biases_sb[:, D:D + E], ALU.add
                                  ).then_inc(route, 1)
                dve.wait_ge(route, base + 1)
                hold_here()
                dve.max(w.top, w.logits).then_inc(route, 1)
                dve.wait_ge(route, base + 2)
                hold_here()
                dve.max_index(w.top_at, w.top, w.logits).then_inc(route, 1)
                dve.tensor_scalar(w.top_gap, w.top[:, 1:2], w.top[:, 0:1], None, ALU.subtract).then_inc(route, 1)
                dve.wait_ge(route, base + 3)
                dve.tensor_copy(w.top_id, w.top_at[:, 0:2]).then_inc(route, 1)

            def gate_inputs(g, w):
                base = GATE * g
                dve.wait_ge(gap_exp, g + 1)
                dve.tensor_scalar(w.gate_den, w.exp_gap, 1.0, None, ALU.add).then_inc(gate, 1)
                dve.wait_ge(gate, base + 1)
                dve.reciprocal(w.gate_of[:, 0:1], w.gate_den).then_inc(gate, 1)
                dve.wait_ge(gate, base + 2)
                dve.tensor_scalar(w.gate_of[:, 1:2], w.gate_of[:, 0:1], w.exp_gap, None, ALU.mult).then_inc(gate, 1)
                dve.wait_ge(route, ROUTE * (g + 1))
                dve.wait_ge(gate, base + 3)
                for n in range(2):
                    dve.tensor_scalar(w.gates2[:, n, :], expert_ids_sb[:], w.top_id[:, n:n + 1],
                                      w.gate_of[:, n:n + 1], ALU.is_equal, ALU.mult).then_inc(gate, 1)
                dve.wait_ge(gate, base + 5)
                dve.tensor_tensor(w.gates, w.gates2[:, 0, :], w.gates2[:, 1, :], ALU.add).then_inc(gate, 1)
                dve.wait_ge(gate, base + 6)
                dve.tensor_tensor(w.gated, w.bank[:, D:D + E * R].rearrange("p (e r) -> p e r", e=E),
                                  w.gates.unsqueeze(2).to_broadcast([P, E, R]), ALU.mult).then_inc(gate, 1)

            def store_gatedT(g, w):
                dve.wait_ge(gatedT_psum, g + 1)
                dve.tensor_copy(w.gatedT, w.turn_bank).then_inc(gatedT_ready, 1)

            def finish(g, w):
                dve.wait_ge(out_psum, g + 1)
                dve.wait_ge(yb_ready, g + 1)
                if w is loop:
                    dve.wait_ge(result_out, 16 * (g + 1))
                dve.tensor_tensor(w.result, w.bank[:, 0:D], w.yb, ALU.add).then_inc(result_ready, 1)

            POST = {"turn_sums": divide, "turn_back": store_attn_t, "o": residual_and_stats,
                    "normalise": normalise_y, "turn": store_yT, "ffn": route_tokens, "gates": gate_inputs,
                    "turn_gated": store_gatedT, "lora": finish}

            PRE = {"turn": store_xT, "project": split_qk, "norm": read_norms}

            GEN_STEPS, GEN_SPLIT = 4, 3
            gen_step = [sem(f"gen_step{c}") for c in range(NCHUNK)]

            project_first_chunk()
            decide_bound(0, 0)
            split_qk(TPC)

            def open_chunk(c):
                dve.wait_ge(bound_step, BOUND_STEPS * (1 + NQUAD * c))
                bounded = dve.value_load(is_bounded[0:1, c:c + 1], min_val=0, max_val=1)
                with dve.If(bounded == 0):
                    shifts(c)

            def serve_quad(c, i):
                pre = pre_slots(c, i)
                for k in range(1, periods[c] + LAG):
                    if TPC * c < k <= periods[c]:
                        clear_later_keys(c, i, k - 1)
                    if k == 1 and pre:
                        measure_x(next_tile(c, i))
                        normalise_x(next_tile(c, i))
                    if k == periods[c] and isinstance(i, int) and c + 1 < NCHUNK:
                        open_chunk(c + 1)
                    if k == DECIDE_AT[c]:
                        decide_bound(c + 1, NQUAD * c + i + 1)
                    for name in pre.get(k, ()):
                        PRE[name](next_tile(c, i))
                    for name in POST_SLOTS[c].get(k, ()):
                        POST[name](TPC * (c - 1) + i, loop)
                keep_sums(c, i)

            open_chunk(0)
            read_norms(TPC)
            for c in range(NCHUNK):
                if c + 2 < NCHUNK:
                    dve.wait_ge(x_in[c + 2], 16)
                if c == 1:
                    dve.wait_ge(post_weights_in, 16 * 4)
                for_quads(dve, c, serve_quad, peel_last=c + 1 < NCHUNK)
            for name, t in TAIL_ORDER:
                if name not in ("turn_back", "turn", "turn_gated"):
                    POST[name](TILES - TPC + t, tail[t])

        @block.gpsimd
        def _(pool):
            def rstd_x(g):
                pool.wait_ge(stats1, STATS1 * (g - TPC + 1))
                pool.tensor_tensor(rstd1[:], ve1[:], minus_half[:, 0:1], ALU.pow).then_inc(rstd1_ready, 1)

            def low_parts(g):
                pool.wait_ge(split, SPLIT * (g - TPC) + 3)
                pool.tensor_tensor(parts[:, :, 2], rest1[:], parts[:, :, 1], ALU.subtract).then_inc(low_ready, 1)

            def gather_sums(g, c, i):
                pool.wait_ge(acc_read, NQUAD * (c + 1) + 1)
                pool.tensor_copy(attn_in[:].unsqueeze(2 if c % 2 == 0 else 1), sums_of_tile(c, i)
                                 ).then_inc(attn_in_ready, 1)

            def rstd_y(g, w):
                pool.wait_ge(stats2, STATS2 * (g + 1))
                pool.tensor_tensor(w.rstd2, w.ve2, minus_half[:, 0:1], ALU.pow).then_inc(rstd2_ready, 1)
                pool.tensor_tensor(w.yb, w.y, biases_sb[:, 0:D], ALU.add).then_inc(yb_ready, 1)

            pool.memset(v_ring[:].rearrange("p n h d -> p (n h d)"), 1.0).then_inc(ones_set, 1)
            pool.wait_ge(ones_set, 1)
            pool.wait_ge(first_stats, 2 * TPC + 1)
            pool.tensor_tensor(first_scale[:], first_ve[:].rearrange("p t o -> p (t o)"), minus_half[:],
                               ALU.pow).then_inc(first_scale_ready, 1)

            rstd_x(TPC)
            low_parts(TPC)

            def serve_quad(c, i):
                pre, post_ = pre_slots(c, i), POST_SLOTS[c]
                first = c == 0 and isinstance(i, int)
                pool.wait_ge(v_stored, TPC * (c + 1))
                for kb in range(periods[c]):
                    n = first_period[c] + i * periods[c] + kb
                    if not (first and kb < V_RING):
                        pool.wait_ge(pv_done, n - V_RING + 1)
                    pool.tensor_copy(v_ring[:, kb % V_RING, :, 0:DK], v_all[:, kb, bass.ds(i * QUAD, QUAD), :]
                                     ).then_inc(v_ready, 1)
                    if kb == RSTD_AT and pre:
                        rstd_x(next_tile(c, i))
                    if kb == GATHER_AT and post_:
                        gather_sums(TPC * (c - 1) + i, c - 1, i)
                    if "o" in post_.get(kb, ()):
                        rstd_y(TPC * (c - 1) + i, loop)
                    if "project" in pre.get(kb, ()):
                        low_parts(next_tile(c, i))

            serve_quad(0, 0)
            with pool.Fori(1, NQUAD) as i:
                serve_quad(0, i)
            for c in range(1, NCHUNK):
                if c == 1:
                    pool.wait_ge(result_out, 16)
                for_quads(pool, c, serve_quad)
            for t, w in enumerate(tail):
                rstd_y(TILES - TPC + t, w)


def kernel(**inputs):
    import concourse.bacc as bacc
    from concourse.bass_utils import run_bass_kernel_spmd

    from ml_dtypes import bfloat16 as bf16

    given = {name: np.asarray(a) for name, a in inputs.items()}

    def halves(w):
        return np.ascontiguousarray(w.reshape(KH, P, w.shape[1]).transpose(1, 0, 2))

    order = np.arange(D).reshape(H, KH, DK // KH).transpose(1, 2, 0).reshape(D)
    wq, wk, wv = (given[f"L0_attn_{n}_proj"] for n in "qkv")
    wo = given["L0_attn_o_proj"]
    row = np.arange(P)
    tail = np.zeros((TAIL, H, CHUNK), np.float32)
    k_tail, q_tail = tail.copy(), tail.copy()
    k_tail[0:SHIFT_ROWS] = 1.0
    q_tail[0] = -SHIFT
    arrays = {
        "x": np.ascontiguousarray(given["L0_attn_in_features"].reshape(TILES, P, D).transpose(1, 0, 2)),
        "wqkv": halves(np.concatenate([wq[order].T, wk[order].T, wv.T], 1)),
        "wo": halves(wo.T),
        "wffn": halves(np.concatenate([given["L0_ffn_W"].T, given["L0_ffn_lora_A"].reshape(E * R, D).T,
                                       given["L0_ffn_gate_w"].T], 1)),
        "lora_b": np.ascontiguousarray(given["L0_ffn_lora_B"].transpose(0, 2, 1).reshape(E * R, D)),
        "biases": np.ascontiguousarray(np.broadcast_to(
            np.concatenate([given["L0_ffn_b"], given["L0_ffn_gate_b"]])[None], (P, D + E))),
        "ident": np.eye(P, dtype=np.float32),
        "ident_bf": np.eye(P, dtype=np.float32).astype(bf16),
        "masks": np.stack([np.where(row[None, :] >= row[:, None], BIG, 0.0),
                           np.where(row[None, :] <= row[:, None], BIG, -BIG)], 1).astype(np.float32),
        "head_sum": (row[:, None] % H == np.arange(H)[None, :]).astype(np.float32).astype(bf16),
        "expert_ids": np.broadcast_to(np.arange(E, dtype=np.float32)[None], (P, E)).copy(),
        "k_tail": k_tail.astype(bf16),
        "q_tail": q_tail.astype(bf16),
    }
    nc = bacc.Bacc("TRN2", target_bir_lowering=False, num_devices=1)
    args = [nc.dram_tensor(n, a.shape, mybir.dt.from_np(a.dtype), kind="ExternalInput").ap()
            for n, a in arrays.items()]
    out = nc.dram_tensor("out", (TILES, P, D), F32, kind="ExternalOutput").ap()
    transformer_block(nc, *args, out)
    r = run_bass_kernel_spmd(nc, [arrays], core_ids=[0])
    return r.results[0]["out"].reshape(1, S, D)
```
